# Optimizing a Trainium2 kernel written in Bass

```python
import numpy as np
import jax
import jax.numpy as jnp

def _softmax(x, axis=-1):
    return jax.nn.softmax(x, axis=axis)

def _gelu(x):
    return jax.nn.gelu(x, approximate=True)

def _silu(x):
    return jax.nn.silu(x)

def _sigmoid(x):
    return jax.nn.sigmoid(x)

def _layernorm(x, axis=-1, eps=1e-05):
    m = jnp.mean(x, axis=axis, keepdims=True)
    v = jnp.var(x, axis=axis, keepdims=True)
    return (x - m) / jnp.sqrt(v + eps)

def _scatter_add(tgt, idx, src, axis=0):
    return tgt.at[idx].add(src)

def _segment_sum(src, seg, n):
    return jax.ops.segment_sum(src, seg, n)
kernel_name = 'mk_vit_tower_postln_d1_tok_img256_r4_00addf'

def setup_inputs(seed: int=0):
    np.random.seed(seed)
    _w = jnp.asarray

    def _rec_inputs():
        import jax
        import jax.numpy as jnp
        _rk = jax.random.key(seed)
        x = -7.10856e-05 + 0.999911 * jax.random.normal(jax.random.fold_in(_rk, 1), (4, 64, 128, 64), jnp.float32)
        return x
    x = _rec_inputs()

    def _L0_tok_setup():
        import jax, jax.numpy as jnp
        import numpy as np
        PATCH_LEN = 16
        STRIDE = 8
        PAD = 8
        key = jax.random.key(seed)
        k1, k2 = jax.random.split(key)
        x = jax.random.normal(k1, (32, 64, 128, 64), dtype=jnp.float32)
        in_feat = 64 * (PATCH_LEN // 2 + 1) * 2
        W = jax.random.normal(k2, (64, in_feat), dtype=jnp.float32) * 0.02
        return {'x': x, 'W': W}
    _L0_tok_all = _L0_tok_setup()
    _L0_tok_in = {k: v for k, v in _L0_tok_all.items() if k in ('W',)}
    del _L0_tok_all

    def _L0_attn_setup():
        import jax, jax.numpy as jnp
        import numpy as np
        DIM = 64
        HEADS = 4
        HEAD_DIM = DIM // HEADS
        SCALE = HEAD_DIM ** (-0.5)
        key = jax.random.key(seed)
        ks = jax.random.split(key, 9)
        B, N, C = (2, 1024, DIM)
        x = jax.random.normal(ks[0], (B, N, C), dtype=jnp.float32)
        lim = np.sqrt(6.0 / (C + C)).astype(np.float32)

        def w(k):
            return jax.random.uniform(k, (C, C), dtype=jnp.float32, minval=-lim, maxval=lim)
        return {'x': x, 'Wq': w(ks[1]), 'bq': jnp.zeros((C,), jnp.float32), 'Wk': w(ks[2]), 'bk': jnp.zeros((C,), jnp.float32), 'Wv': w(ks[3]), 'bv': jnp.zeros((C,), jnp.float32), 'Wo': w(ks[4]), 'bo': jnp.zeros((C,), jnp.float32)}
    _L0_attn_all = _L0_attn_setup()
    _L0_attn_in = {k: v for k, v in _L0_attn_all.items() if k in ('Wq', 'bq', 'Wk', 'bk', 'Wv', 'bv', 'Wo', 'bo')}
    del _L0_attn_all

    def _L0_ffn_setup():
        import jax, jax.numpy as jnp
        import numpy as np
        B, A = (1024, 8)
        IN, OUT = (64, 64)
        SH1, SH2 = (64, 128)
        EH1, EH2 = (128, 64)
        E, TOPK = (4, 2)

        def _shared_mlp(x, W1, b1, W2, b2, W3, b3):
            h = jax.nn.relu(x @ W1 + b1)
            h = jax.nn.relu(h @ W2 + b2)
            return h @ W3 + b3

        def _experts_mlp(x, eW1, eb1, eW2, eb2, eW3, eb3):
            h = jax.nn.relu(jnp.einsum('baf,efh->ebah', x, eW1) + eb1[:, None, None, :])
            h = jax.nn.relu(jnp.einsum('ebah,ehg->ebag', h, eW2) + eb2[:, None, None, :])
            o = jnp.einsum('ebag,ego->ebao', h, eW3) + eb3[:, None, None, :]
            return jnp.moveaxis(o, 0, -1)
        key = jax.random.key(seed)
        ks = jax.random.split(key, 16)
        s = 0.05
        return {'x': jax.random.normal(ks[0], (B, A, IN), jnp.float32), 'sW1': jax.random.normal(ks[1], (IN, SH1), jnp.float32) * s, 'sb1': jnp.zeros((SH1,), jnp.float32), 'sW2': jax.random.normal(ks[2], (SH1, SH2), jnp.float32) * s, 'sb2': jnp.zeros((SH2,), jnp.float32), 'sW3': jax.random.normal(ks[3], (SH2, OUT), jnp.float32) * s, 'sb3': jnp.zeros((OUT,), jnp.float32), 'eW1': jax.random.normal(ks[4], (E, IN, EH1), jnp.float32) * s, 'eb1': jnp.zeros((E, EH1), jnp.float32), 'eW2': jax.random.normal(ks[5], (E, EH1, EH2), jnp.float32) * s, 'eb2': jnp.zeros((E, EH2), jnp.float32), 'eW3': jax.random.normal(ks[6], (E, EH2, OUT), jnp.float32) * s, 'eb3': jnp.zeros((E, OUT), jnp.float32), 'gW': jax.random.normal(ks[7], (IN, E), jnp.float32) * s, 'gb': jnp.zeros((E,), jnp.float32)}
    _L0_ffn_all = _L0_ffn_setup()
    _L0_ffn_in = {k: v for k, v in _L0_ffn_all.items() if k in ('sW1', 'sb1', 'sW2', 'sb2', 'sW3', 'sb3', 'eW1', 'eb1', 'eW2', 'eb2', 'eW3', 'eb3', 'gW', 'gb')}
    del _L0_ffn_all
    return {'x': x, 'L0_tok_W': _L0_tok_in['W'], 'L0_attn_Wq': _L0_attn_in['Wq'], 'L0_attn_bq': _L0_attn_in['bq'], 'L0_attn_Wk': _L0_attn_in['Wk'], 'L0_attn_bk': _L0_attn_in['bk'], 'L0_attn_Wv': _L0_attn_in['Wv'], 'L0_attn_bv': _L0_attn_in['bv'], 'L0_attn_Wo': _L0_attn_in['Wo'], 'L0_attn_bo': _L0_attn_in['bo'], 'L0_ffn_sW1': _L0_ffn_in['sW1'], 'L0_ffn_sb1': _L0_ffn_in['sb1'], 'L0_ffn_sW2': _L0_ffn_in['sW2'], 'L0_ffn_sb2': _L0_ffn_in['sb2'], 'L0_ffn_sW3': _L0_ffn_in['sW3'], 'L0_ffn_sb3': _L0_ffn_in['sb3'], 'L0_ffn_eW1': _L0_ffn_in['eW1'], 'L0_ffn_eb1': _L0_ffn_in['eb1'], 'L0_ffn_eW2': _L0_ffn_in['eW2'], 'L0_ffn_eb2': _L0_ffn_in['eb2'], 'L0_ffn_eW3': _L0_ffn_in['eW3'], 'L0_ffn_eb3': _L0_ffn_in['eb3'], 'L0_ffn_gW': _L0_ffn_in['gW'], 'L0_ffn_gb': _L0_ffn_in['gb']}

def reference(x, L0_tok_W, L0_attn_Wq, L0_attn_bq, L0_attn_Wk, L0_attn_bk, L0_attn_Wv, L0_attn_bv, L0_attn_Wo, L0_attn_bo, L0_ffn_sW1, L0_ffn_sb1, L0_ffn_sW2, L0_ffn_sb2, L0_ffn_sW3, L0_ffn_sb3, L0_ffn_eW1, L0_ffn_eb1, L0_ffn_eW2, L0_ffn_eb2, L0_ffn_eW3, L0_ffn_eb3, L0_ffn_gW, L0_ffn_gb):
    import jax
    import jax.numpy as jnp

    def _L0_tok_ref(x, W):
        import jax, jax.numpy as jnp
        import numpy as np
        PATCH_LEN = 16
        STRIDE = 8
        PAD = 8
        B, C, T, V = x.shape
        xp = jnp.pad(x, ((0, 0), (0, 0), (0, PAD), (0, 0)), mode='edge')
        Tp = T + PAD
        N = (Tp - PATCH_LEN) // STRIDE + 1
        idx = jnp.arange(N)[:, None] * STRIDE + jnp.arange(PATCH_LEN)[None, :]
        patches = xp[:, :, idx, :]
        patches = jnp.transpose(patches, (0, 4, 2, 3, 1))
        xf = jnp.fft.rfft(patches, axis=-2, norm='ortho')
        F = xf.shape[-2]
        x_real = xf.real.reshape(B, V, N, F * C)
        x_imag = xf.imag.reshape(B, V, N, F * C)
        x_emb = jnp.concatenate([x_real, x_imag], axis=-1)
        x_emb = x_emb @ W.T
        return x_emb.reshape(B, V * N, -1)

    def _L0_attn_ref(x, Wq, bq, Wk, bk, Wv, bv, Wo, bo):
        import jax, jax.numpy as jnp
        import numpy as np
        DIM = 64
        HEADS = 4
        HEAD_DIM = DIM // HEADS
        SCALE = HEAD_DIM ** (-0.5)
        B, N, C = x.shape
        x = jnp.clip(x, -10000.0, 10000.0)

        def heads(t):
            return t.reshape(B, N, HEADS, HEAD_DIM).transpose(0, 2, 1, 3)
        q = heads((x @ Wq.T + bq).astype(jnp.float32))
        k = heads((x @ Wk.T + bk).astype(jnp.float32))
        v = heads((x @ Wv.T + bv).astype(jnp.float32))
        attn = jnp.einsum('bhnd,bhmd->bhnm', q, k) * SCALE
        attn = jax.nn.softmax(attn, axis=-1)
        out = jnp.einsum('bhnm,bhmd->bhnd', attn, v)
        out = out.transpose(0, 2, 1, 3).reshape(B, N, C)
        out = out.astype(jnp.bfloat16).astype(jnp.float32)
        return out @ Wo.T + bo

    def _L0_ffn_ref(x, sW1, sb1, sW2, sb2, sW3, sb3, eW1, eb1, eW2, eb2, eW3, eb3, gW, gb):
        import jax, jax.numpy as jnp
        import numpy as np
        B, A = (1024, 8)
        IN, OUT = (64, 64)
        SH1, SH2 = (64, 128)
        EH1, EH2 = (128, 64)
        E, TOPK = (4, 2)

        def _shared_mlp(x, W1, b1, W2, b2, W3, b3):
            h = jax.nn.relu(x @ W1 + b1)
            h = jax.nn.relu(h @ W2 + b2)
            return h @ W3 + b3

        def _experts_mlp(x, eW1, eb1, eW2, eb2, eW3, eb3):
            h = jax.nn.relu(jnp.einsum('baf,efh->ebah', x, eW1) + eb1[:, None, None, :])
            h = jax.nn.relu(jnp.einsum('ebah,ehg->ebag', h, eW2) + eb2[:, None, None, :])
            o = jnp.einsum('ebag,ego->ebao', h, eW3) + eb3[:, None, None, :]
            return jnp.moveaxis(o, 0, -1)
        all_out = _experts_mlp(x, eW1, eb1, eW2, eb2, eW3, eb3)
        shared = _shared_mlp(x, sW1, sb1, sW2, sb2, sW3, sb3)
        gates = jax.nn.softmax(x @ gW + gb, axis=-1)
        topv, topi = jax.lax.top_k(gates, TOPK)
        topw = jax.nn.softmax(topv, axis=-1)
        sel = jnp.take_along_axis(all_out, topi[:, :, None, :], axis=-1)
        gated = jnp.sum(sel * topw[:, :, None, :], axis=-1)
        return shared + gated
    h = _L0_tok_ref(x, L0_tok_W)
    h = _layernorm(h + _L0_attn_ref(h, L0_attn_Wq, L0_attn_bq, L0_attn_Wk, L0_attn_bk, L0_attn_Wv, L0_attn_bv, L0_attn_Wo, L0_attn_bo), axis=-1)
    h = _layernorm(h + _L0_ffn_ref(h, L0_ffn_sW1, L0_ffn_sb1, L0_ffn_sW2, L0_ffn_sb2, L0_ffn_sW3, L0_ffn_sb3, L0_ffn_eW1, L0_ffn_eb1, L0_ffn_eW2, L0_ffn_eb2, L0_ffn_eW3, L0_ffn_eb3, L0_ffn_gW, L0_ffn_gb), axis=-1)
    return h

_drawn_inputs = setup_inputs


def setup_inputs(seed=0):
    import zlib

    import numpy as np

    out = dict(_drawn_inputs(seed))
    spreads = {'L0_attn_bq': (0.0, 0.8),
     'L0_attn_bk': (0.0, 0.8),
     'L0_attn_bv': (0.0, 0.1),
     'L0_attn_bo': (0.0, 0.1),
     'L0_ffn_sb1': (0.0, 0.729),
     'L0_ffn_sb2': (0.0, 0.1),
     'L0_ffn_sb3': (0.0, 0.1),
     'L0_ffn_eb1': (0.0, 0.8),
     'L0_ffn_eb2': (0.0, 0.534),
     'L0_ffn_eb3': (0.0, 0.1),
     'L0_ffn_gb': (0.0, 0.305)}
    factors = {'L0_ffn_eW1': 2.703}
    for name, (base, spread) in spreads.items():
        noise = np.random.default_rng([zlib.crc32(name.encode()), seed]).standard_normal(out[name].shape)
        drawn = base * np.exp(spread * noise) if base else spread * noise
        out[name] = jnp.asarray(drawn.astype(out[name].dtype))
    for name, factor in factors.items():
        out[name] = (out[name] * factor).astype(out[name].dtype)
    return out
```

```python
from contextlib import ExitStack

import concourse.bass as bass
from concourse import mybir

F32 = mybir.dt.float32
BF16 = mybir.dt.bfloat16
ALU = mybir.AluOpType
ACT = mybir.ActivationFunctionType
AX = mybir.AxisListType

B, C, T, V = 4, 64, 128, 64
PATCH, STRIDE, NPATCH = 16, 8, 16
RF = PATCH + 2
CG = 4
N = V * NPATCH
D, H, DH = 64, 4, 16
NT = N // 128
HALF = N // 2
E = 4
SCALE = float(DH) ** -0.5
CLIP = 10000.0
EPS = 1e-5
TERMS_Q = (0, 0, 0, 1, 1, 2)
TERMS_K = (0, 1, 2, 0, 1, 0)
KS = 16 * len(TERMS_Q)
KM = KS + 3
KW = 96

PACK, _at = {}, 0
for _name, _rows, _cols in (
    ("ident", 128, 128), ("wqk", KW, 128), ("wv", KW, 64), ("wo", 128, 64), ("bo", 128, 1),
    ("s1", KW, 64 + E), ("e1", KW, 128 * E), ("s2", KW, 128), ("e2", 128, 64 * E), ("eb2", 128, 2),
    ("w3", KW + E, 64), ("s3", 128, 64), ("e3", 128, 128), ("dft", KW, CG * PATCH), ("wt", KW, 16 * 64),
):
    PACK[_name] = (_rows, _at, _cols)
    _at += _cols
PACK_COLS = _at

SM_SEQ = [("tok",), ("v",)] + [("sm", 0, m, c) for m in range(NT) for c in range(2)]
_sm1 = [("sm", 1, m, c) for m in range(NT) for c in range(2)]
SM_SEQ += _sm1[:2] + [("t", 0)] + _sm1[2:] + [("t", 1)]
for _h in (2, 3):
    SM_SEQ += [("sm", _h, m, c) for m in range(NT) for c in range(2)] + [("t", _h)]
SM_AT = {k: n for n, k in enumerate(SM_SEQ)}
SM_LEN = len(SM_SEQ)
R_SEQ = [("st", h, m, c) for h in range(H) for m in range(NT) for c in range(2)]
FFN_STEPS = [("s1", 0), ("s1", 1)] + [(k, ch) for ch in range(2) for k in ("e0", "e1", "e2", "e3", "s2", "p0", "p1")]
R_SEQ += FFN_STEPS + [("l3",)]
R_AT = {k: n for n, k in enumerate(R_SEQ)}
R_LEN = len(R_SEQ)
assert SM_LEN % 2 == 0 and R_LEN % 3 == 0
M_SEQ = ["t01", "t23", "aot", "wo", "r1t", "h1t", "gl", "gt", "r2t"]
M_AT = {k: n for n, k in enumerate(M_SEQ)}
FIRST_MAX = SM_SEQ[2:2 + 25]
AHEAD0 = 6
AHEAD = {n: (2 * (n - AHEAD0), 2 * (n - AHEAD0 + 1)) for n in range(AHEAD0, len(FFN_STEPS))}
AHEAD[len(FFN_STEPS) - 1] = (18, 19)
GATES_AT = 8
_rest = SM_SEQ[2 + 25:]
BESIDE = {}
for _h in range(3):
    for _m in range(NT):
        _n = (0 if _m > 3 and _h == 2 else 2) + (_m == 4)
        BESIDE[_h, _m], _rest = _rest[:_n], _rest[_n:]
assert not _rest and all(BESIDE[_h, 4][0] == ("t", _h + 1) for _h in range(3))
DVE_STEPS = 34
M_LEN = len(M_SEQ)
NPT = 4


def vit_layer(nc, x, pack, out):
    with ExitStack() as ctx:
        def sb(name, shape, dt=F32):
            return ctx.enter_context(nc.sbuf_tensor(name, shape, dt))

        def sem(name):
            return ctx.enter_context(nc.semaphore(name))

        banks = [ctx.enter_context(nc.psum_tensor(f"bank{i}", [128, 512], F32)) for i in range(8)]
        sm_bank, r_bank, ot_bank, m_bank = banks[0:2], banks[2:5], banks[5:7], banks[7]
        m_bf = m_bank[:, :].bitcast(BF16)

        qk_dram = nc.dram_tensor("qk_dram", (2, 64, 3, N), BF16)
        mx_dram = nc.dram_tensor("mx_dram", (H, NT, 3, 128), BF16)
        gate_dram = nc.dram_tensor("gate_dram", (E, N), F32)

        pk = sb("pk", [128, PACK_COLS])

        def w(name, r0=0, r1=None):
            rows, at, cols = PACK[name]
            return pk[r0:rows if r1 is None else r1, at:at + cols]

        ident = w("ident")
        ident_bf = sb("ident_bf", [128, 128], BF16)
        mt = sb("mt", [64, CG * 16 * PATCH])
        wtok = sb("wtok", [128, 8, 64])
        xs = sb("xs", [128, NPATCH + 1, 4 * V])
        comb = sb("comb", [128, N])
        hc = sb("hc", [KW, N])
        vv = sb("vv", [128, NT, H, 32])
        parts = sb("parts", [128, 3, N], BF16)
        rest = sb("rest", [128, N])
        qst = sb("qst", [KM, H, N], BF16)
        kst = sb("kst", [KM, H, N], BF16)
        pt = sb("pt", [128, NPT, N])
        mx2 = sb("mx2", [128, H, NT, 2])
        ngm = sb("ngm", [128, H, NT])
        mrest = sb("mrest", [NT, 128])
        mpart = sb("mpart", [NT, 2, 3, 128], BF16)
        osb = sb("osb", [128, H, 256])
        rec = sb("rec", [128, 2, 2, 8])
        ao = sb("ao", [128, NT, D], BF16)
        r1 = sb("r1", [128, HALF])
        r2 = sb("r2", [128, HALF])
        xc = sb("xc", [128, NT, D])
        sq = sb("sq", [128, NT, D])
        st = sb("st", [128, 5, NT])
        halfpow = sb("halfpow", [128, NT])
        h1 = sb("h1", [128, NT, D])
        h1t = sb("h1t", [KW + E, N])
        y = sb("y", [128, NT, D])
        s1o = sb("s1o", [KW, 2, HALF])
        logits = sb("logits", [E, N])
        s2o = sb("s2o", [128, 2, HALF])
        e1o = sb("e1o", [128, 2, E, HALF])
        e2o = sb("e2o", [128, 2, 2, HALF])
        e2g = sb("e2g", [128, 2, 2, HALF])
        wgb = sb("wgb", [128, 2, N])
        gl = sb("gl", [128, NT, E])
        gd = sb("gd", [128, NT, E])
        ge = sb("ge", [128, NT, E])
        gp = sb("gp", [128, NT, E])
        gu = sb("gu", [128, NT, E])
        later = sb("later", [128, NT, E])
        rank = sb("rank", [128, NT, E])
        gm = sb("gm", [128, NT, E])
        gc = sb("gc", [128, E, NT, E])
        gs = sb("gs", [128, 6, NT])
        gw = sb("gw", [128, E, NT])
        gwt = sb("gwt", [E * NT, 128])

        packed, x_in, stack_in, mrow_out, mrow_in = (sem(n) for n in ("packed", "x_in", "stack_in", "mrow_out", "mrow_in"))
        parts_out, gate_out, gate_in, y_out = (sem(n) for n in ("parts_out", "gate_out", "gate_in", "y_out"))
        ones_set, ident_set, mt_full, mt_read, wt_full, wt_read, pool_set = (
            sem(n) for n in ("ones_set", "ident_set", "mt_full", "mt_read", "wt_full", "wt_read", "pool_set"))
        sm_full, sm_free, r_full, r_free, m_full = (sem(n) for n in ("sm_full", "sm_free", "r_full", "r_free", "m_full"))
        qk_full, p1_done, rest_done, p2_done, p3_done = (
            sem(n) for n in ("qk_full", "p1_done", "rest_done", "p2_done", "p3_done"))
        raw_done, hc_done, pv_done, osb_done, ao_done = (
            sem(n) for n in ("raw_done", "hc_done", "pv_done", "osb_done", "ao_done"))
        max_done, mpart_done, comb_done, r1_done = (sem(n) for n in ("max_done", "mpart_done", "comb_done", "r1_done"))
        xc_done, sq_done, var_done, rstd_done, h1_done, h1t_done, y_done = (
            sem(n) for n in ("xc_done", "sq_done", "var_done", "rstd_done", "h1_done", "h1t_done", "y_done"))
        logits_done = sem("logits_done")
        gl_done, gd_done, ge_done, gu_done, gw_done, gwt_done, e2g_done = (
            sem(n) for n in ("gl_done", "gd_done", "ge_done", "gu_done", "gw_done", "gwt_done", "e2g_done"))
        dve_step = sem("dve_step")

        block = ctx.enter_context(nc.Block())

        x_v = x.rearrange("b c (n g j) v -> b g c n (j v)", n=NPATCH, g=2, j=4)
        x_last = x[:, :, T - 1, :]
        out_v = out.rearrange("b (v g i) o -> b g v (i o)", v=V, g=2, i=NT)

        @block.sync
        def _(sp):
            def load_x(b):
                for g in range(2):
                    sp.dma_start(xs[64 * g:64 * g + 64, 0:NPATCH, :], x_v[b, g]).then_inc(x_in, 16)
                    for j in range(4):
                        sp.dma_start(xs[64 * g:64 * g + 64, NPATCH, V * j:V * j + V], x_last[b]).then_inc(x_in, 16)

            def stacks(b):
                sp.wait_ge(p3_done, 2 * b + 2)
                sp.wait_ge(p2_done, 2 * b + 2)
                sp.dma_start(qk_dram.ap().rearrange("s r t n -> (s r) t n"), parts[:, :, :]).then_inc(parts_out, 16)
                sp.wait_ge(parts_out, 16 * (b + 1))
                for side, (dst, terms) in enumerate(((qst, TERMS_Q), (kst, TERMS_K))):
                    for t, part in enumerate(terms):
                        sp.dma_start(dst[16 * t:16 * t + 16, :, :],
                                     qk_dram[side, :, part, :].rearrange("(d h) n -> d h n", h=H)).then_inc(stack_in, 16)

            def max_rows(b, h):
                sp.wait_ge(mpart_done, H * b + h + 1)
                sp.dma_start(mx_dram[h], mpart[:, h % 2, :, :]).then_inc(mrow_out, 16)
                sp.wait_ge(mrow_out, 16 * (H * b + h + 1))
                sp.dma_start(qst[KS:KM, h, :].rearrange("p (j n) -> p j n", j=NT),
                             mx_dram[h].rearrange("j t n -> t j n")).then_inc(mrow_in, 16)

            def gates(b):
                sp.wait_ge(gwt_done, b + 1)
                sp.dma_start(gate_dram.ap().rearrange("e (i n) -> (e i) n", i=NT), gwt[:, :]).then_inc(gate_out, 16)
                sp.wait_ge(gate_out, 16 * (b + 1))
                for e in range(E):
                    sp.dma_start(wgb[64 * (e % 2):64 * (e % 2) + 64, e // 2, :],
                                 gate_dram[e:e + 1, :].to_broadcast([64, N])).then_inc(gate_in, 16)
                sp.dma_start(h1t[KW:KW + E, :], gate_dram.ap()).then_inc(gate_in, 16)

            def store(b):
                sp.wait_ge(y_done, b + 1)
                for g in range(2):
                    sp.dma_start(out_v[b, g], y[64 * g:64 * g + 64, :, :].rearrange("p i o -> p (i o)")).then_inc(y_out, 16)

            def batch(b, last):
                if not last:
                    sp.wait_ge(sm_full, SM_LEN * b + SM_AT[("tok",)] + 1)
                    load_x(b + 1)
                for h in range(1, H):
                    max_rows(b, h)
                if not last:
                    stacks(b + 1)
                gates(b)
                if not last:
                    max_rows(b + 1, 0)
                store(b)

            sp.dma_start(pk[:, :], pack).then_inc(packed, 16)
            load_x(0)
            stacks(0)
            max_rows(0, 0)
            with sp.Fori(0, B - 1) as b:
                batch(b, False)
            batch(B - 1, True)
            sp.wait_ge(y_out, 32 * B + 1)

        @block.gpsimd
        def _(pool):
            for n, (dst, value) in enumerate((
                    (hc[64:KW, :], 0.0), (h1t[64:KW, :], 0.0), (s1o[64:KW, :, :], 0.0),
                    (hc[64:65, :], 1.0), (h1t[64:65, :], 1.0), (s1o[64:65, :, :], 1.0), (vv[:, :, :, 16:32], 1.0),
                    (kst[KS:KM, :, :], 1.0), (halfpow[:, :], -0.5))):
                if n:
                    pool.wait_ge(pool_set, n)
                pool.memset(dst, value).then_inc(pool_set, 1)
            pool.wait_ge(pool_set, 9)

            def third_parts(b):
                for c in range(2):
                    s = slice(c * HALF, (c + 1) * HALF)
                    pool.wait_ge(p2_done, 2 * b + c + 1)
                    pool.tensor_tensor(parts[:, 2, s], rest[:, s], parts[:, 1, s], ALU.subtract).then_inc(p3_done, 1)

            def rstd(n):
                pool.wait_ge(var_done, n + 1)
                pool.tensor_tensor(st[:, 4, :], st[:, 3, :], halfpow[:, :], ALU.pow).then_inc(rstd_done, 1)

            def batch(b, last):
                if not last:
                    rstd(2 * b)
                    third_parts(b + 1)
                else:
                    rstd(2 * b)
                rstd(2 * b + 1)

            third_parts(0)
            with pool.Fori(0, B - 1) as b:
                batch(b, False)
            batch(B - 1, True)

        @block.tensor
        def _(pe):
            def sm_slot(b, key):
                n = SM_AT[key]
                pe.wait_ge(sm_free, SM_LEN * b + n + 1)
                return sm_bank[n % 2]

            def r_slot(b, key):
                n = R_AT[key]
                pe.wait_ge(r_free, R_LEN * b + n + 1)
                return r_bank[n % 3]

            m_read = {"t01": (ao_done, 4, 2), "t23": (ao_done, 4, 4), "aot": (comb_done, 2, 2), "wo": (r1_done, 1, 1),
                      "r1t": (xc_done, 2, 1), "h1t": (h1t_done, 2, 2), "gl": (gl_done, 1, 1), "gt": (gwt_done, 1, 1),
                      "r2t": (xc_done, 2, 2)}

            def m_slot(b, key):
                if key != M_SEQ[0]:
                    who, per, at = m_read[M_SEQ[M_AT[key] - 1]]
                    pe.wait_ge(who, per * b + at)

            def setup():
                pe.wait_ge(packed, 16)
                for g in range(16):
                    mm = pe.matmul(ot_bank[g // 8][0:64, 64 * (g % 8):64 * (g % 8) + 64],
                                   w("wt")[:, 64 * g:64 * g + 64], w("dft"), start=True, stop=True)
                mm.then_inc(mt_full, 1)
                pe.wait_ge(mt_read, 4)
                for kt in range(8):
                    mm = pe.transpose(m_bank[:, 64 * kt:64 * kt + 64], mt[:, 128 * kt:128 * kt + 128], ident[0:64, 0:64])
                mm.then_inc(wt_full, 1)
                pe.wait_ge(wt_read, 1)
                pe.wait_ge(ident_set, 1)
                pe.wait_ge(pool_set, 9)

            def tokens(b, k0=0, k1=8):
                if k0 == 0:
                    sm_slot(b, ("tok",))
                    pe.wait_ge(x_in, 160 * (b + 1))
                bank = sm_bank[0]
                for kt in range(k0, k1):
                    for nn in range(2):
                        n0 = 8 * nn + kt // 4
                        mm = pe.matmul(bank[64 * nn:64 * nn + 64, :], wtok[:, kt, :],
                                       xs[:, n0:n0 + 8, V * (kt % 4):V * (kt % 4) + V],
                                       start=(kt == 0), stop=(kt == 7))
                if k1 == 8:
                    mm.then_inc(sm_full, 1)

            def project(b):
                pe.wait_ge(sm_free, SM_LEN * b + SM_AT[("tok",)] + 3)
                pe.wait_ge(hc_done, b + 1)
                for c in range(2):
                    pe.matmul(ot_bank[c][:, :], w("wqk"), hc[:, c * HALF:(c + 1) * HALF],
                              start=True, stop=True).then_inc(qk_full, 1)
                bank = sm_slot(b, ("v",))
                for i in range(NT):
                    mm = pe.matmul(bank[:, D * i:D * i + D], hc[:, 128 * i:128 * i + 128], w("wv"), start=True, stop=True)
                mm.then_inc(sm_full, 1)

            def max_tile(b, h, m, c):
                bank = sm_slot(b, ("sm", h, m, c))
                pe.matmul(bank[:, :], qst[0:KS, h, 128 * m:128 * m + 128], kst[0:KS, h, c * HALF:(c + 1) * HALF],
                          start=True, stop=True).then_inc(sm_full, 1)

            def max_turn(b, h):
                bank = sm_slot(b, ("t", h))
                pe.wait_ge(max_done, H * b + h + 1)
                pe.transpose(bank[0:NT, 0:128], ngm[:, h, :], ident).then_inc(sm_full, 1)

            def scores(b, h, m):
                for c in range(2):
                    bank = r_slot(b, ("st", h, m, c))
                    pe.matmul(bank[:, :], kst[0:KM, h, 128 * m:128 * m + 128], qst[0:KM, h, c * HALF:(c + 1) * HALF],
                              start=True, stop=True).then_inc(r_full, 1)

            def weigh(b, h, m):
                pe.wait_ge(r_free, R_LEN * b + R_AT[("st", h, m, 1)] + 4)
                for j in range(4):
                    mm = pe.matmul(ot_bank[h % 2][32 * j:32 * j + 32, 0:256], vv[:, m, h, :],
                                   pt[:, m % NPT, 256 * j:256 * j + 256], start=(m == 0), stop=(m == NT - 1),
                                   tile_position=(0, 32 * j))
                mm.then_inc(pv_done, 1)

            def turn_heads(b, p):
                m_slot(b, ("t01", "t23")[p])
                pe.wait_ge(osb_done, H * b + 2 * p + 2)
                for n in range(4):
                    mm = pe.transpose(m_bank[:, 128 * n:128 * n + 128],
                                      osb[:, 2 * p + n // 2, 128 * (n % 2):128 * (n % 2) + 128], ident)
                mm.then_inc(m_full, 1)

            def attention(b):
                pe.wait_ge(sm_free, SM_LEN * b + SM_AT[("v",)] + 3)
                for h in range(H):
                    pe.wait_ge(mrow_in, 16 * (H * b + h + 1))
                    for m in range(NT):
                        scores(b, h, m)
                        maxima(b, BESIDE.get((h, m), ()))
                        if h > 0 and m == 1:
                            weigh_last(b, h - 1)
                        if m >= 2:
                            if m == 2 and h >= 2:
                                pe.wait_ge(osb_done, H * b + h - 1)
                            weigh(b, h, m - 2)
                        if h == 2 and m == 6:
                            turn_heads(b, 0)
                weigh_last(b, H - 1)

            def weigh_last(b, h):
                weigh(b, h, NT - 2)
                weigh(b, h, NT - 1)

            def turn_output(b):
                m_slot(b, "aot")
                pe.wait_ge(ao_done, 4 * b + 4)
                for i in range(NT // 2):
                    mm = pe.transpose(m_bf[:, 128 * i:128 * i + 128],
                                      ao[:, 2 * i:2 * i + 2, :].rearrange("p a o -> p (a o)"), ident_bf[:, :])
                mm.then_inc(m_full, 1)

            def output(b):
                m_slot(b, "wo")
                pe.wait_ge(comb_done, 2 * b + 2)
                for c in range(2):
                    mm = pe.matmul(m_bank[64 * c:64 * c + 64, :], w("wo"), comb[:, c * HALF:(c + 1) * HALF],
                                   start=True, stop=True)
                mm.then_inc(m_full, 1)

            def turn_residual(b, key, src):
                m_slot(b, key)
                if key == "r2t":
                    pe.wait_ge(r_free, R_LEN * b + R_AT[("l3",)] + 4)
                for c in range(4):
                    mm = pe.transpose(m_bank[:, 128 * c:128 * c + 128], src[:, 128 * c:128 * c + 128], ident)
                mm.then_inc(m_full, 1)

            def turn_h1(b):
                m_slot(b, "h1t")
                pe.wait_ge(h1_done, b + 1)
                for c in range(4):
                    mm = pe.transpose(m_bank[:, 128 * c:128 * c + 128],
                                      h1[:, 2 * c:2 * c + 2, :].rearrange("p a o -> p (a o)"), ident)
                mm.then_inc(m_full, 1)

            def turn_logits(b):
                for i in range(NT):
                    mm = pe.transpose(m_bank[:, E * i:E * i + E], logits[:, 128 * i:128 * i + 128], ident[0:E, 0:E])
                mm.then_inc(m_full, 1)

            def turn_gates(b):
                m_slot(b, "gt")
                pe.wait_ge(gw_done, b + 1)
                pe.transpose(m_bank[0:E * NT, 0:128], gw[:, :, :].rearrange("p e i -> p (e i)"), ident).then_inc(m_full, 1)

            def ffn_step(b, kind, ch):
                s = slice(ch * HALF, (ch + 1) * HALF)
                if kind == "s2":
                    pe.wait_ge(r_free, R_LEN * b + R_AT[("e3", ch)] + 4)
                bank = r_slot(b, (kind, ch))
                if kind == "s1":
                    mm = pe.matmul(bank[0:64 + E, :], w("s1"), h1t[0:KW, s], start=True, stop=True)
                elif kind[0] == "e":
                    e = int(kind[1])
                    mm = pe.matmul(bank[:, :], w("e1")[:, 128 * e:128 * e + 128], h1t[0:KW, s], start=True, stop=True)
                elif kind == "s2":
                    mm = pe.matmul(bank[:, :], w("s2"), s1o[:, ch, :], start=True, stop=True)
                else:
                    for k in range(2):
                        e = 2 * int(kind[1]) + k
                        mm = pe.matmul(bank[64 * k:64 * k + 64, :], w("e2")[:, 64 * e:64 * e + 64], e1o[:, ch, e, :],
                                       start=True, stop=True)
                mm.then_inc(r_full, 1)

            def last_layer(b):
                bank = r_slot(b, ("l3",))
                pe.wait_ge(gate_in, 80 * (b + 1))
                pe.wait_ge(r_free, R_LEN * b + R_AT[("p1", 1)] + 4)
                pe.wait_ge(e2g_done, 4 * b + 4)
                for k in range(4):
                    for ch in range(2):
                        lhs = (w("w3"), w("s3"), w("e3")[:, 0:64], w("e3")[:, 64:128])[k]
                        rhs = (h1t[:, ch * HALF:(ch + 1) * HALF], s2o[:, ch, :], e2g[:, ch, 0, :], e2g[:, ch, 1, :])[k]
                        mm = pe.matmul(bank[64 * ch:64 * ch + 64, :], lhs, rhs, start=(k == 0), stop=(k == 3))
                mm.then_inc(r_full, 1)

            def maxima(b, keys):
                for key in keys:
                    if key[0] == "t":
                        max_turn(b, key[1])
                    else:
                        max_tile(b, *key[1:])

            def batch(b, last):
                attention(b)
                if not last:
                    tokens(b + 1, 0, 1)
                turn_heads(b, 1)
                if not last:
                    tokens(b + 1, 1, 2)
                turn_output(b)
                if not last:
                    tokens(b + 1, 2, 4)
                output(b)
                if not last:
                    tokens(b + 1, 4, 5)
                turn_residual(b, "r1t", r1)
                if not last:
                    tokens(b + 1, 5, 8)
                if not last:
                    project(b + 1)
                turn_h1(b)
                pe.wait_ge(h1t_done, 2 * b + 2)
                for n, (kind, ch) in enumerate(FFN_STEPS):
                    if n == 3:
                        pe.wait_ge(logits_done, 2 * b + 2)
                    ffn_step(b, kind, ch)
                    if n == 3:
                        turn_logits(b)
                    if n == GATES_AT:
                        turn_gates(b)
                    if not last and n >= AHEAD0:
                        if n == AHEAD0:
                            pe.wait_ge(stack_in, 192 * (b + 2))
                        maxima(b + 1, FIRST_MAX[slice(*AHEAD[n])])
                if not last:
                    maxima(b + 1, FIRST_MAX[19:22])
                last_layer(b)
                turn_residual(b, "r2t", r2)
                if not last:
                    maxima(b + 1, FIRST_MAX[22:])

            setup()
            tokens(0)
            project(0)
            pe.wait_ge(stack_in, 192)
            maxima(0, FIRST_MAX)
            with pe.Fori(0, B - 1) as b:
                batch(b, False)
            batch(B - 1, True)

        @block.scalar
        def _(act):
            def raw_tokens(b):
                act.wait_ge(sm_full, SM_LEN * b + SM_AT[("tok",)] + 1)
                for nn in range(2):
                    dst = comb[64:128, :].rearrange("p (i g v) -> p g i v", g=2, v=V)[:, nn]
                    act.activation(dst, sm_bank[0][64 * nn:64 * nn + 64, :].rearrange("p (i v) -> p i v", v=V),
                                   ACT.Copy).then_inc(raw_done, 1)

            def first_parts(b):
                for c in range(2):
                    act.wait_ge(qk_full, 2 * b + c + 1)
                    act.activation(parts[:, 0, c * HALF:(c + 1) * HALF], ot_bank[c][:, :], ACT.Copy).then_inc(p1_done, 1)

            def exponentials(b):
                for h in range(H):
                    for m in range(NT):
                        if h or m >= NPT:
                            act.wait_ge(pv_done, H * NT * b + NT * h + m - NPT + 1)
                        for c in range(2):
                            n = R_AT[("st", h, m, c)]
                            act.wait_ge(r_full, R_LEN * b + n + 1)
                            act.activation(pt[:, m % NPT, c * HALF:(c + 1) * HALF], r_bank[n % 3][:, :], ACT.Exp,
                                           scale=SCALE).then_inc(r_free, 1)

            def output(b):
                act.wait_ge(m_full, M_LEN * b + M_AT["aot"] + 1)
                for k in range(2):
                    act.activation(comb[0:64, :].rearrange("p (i k n) -> p k i n", k=2, n=128)[:, k],
                                   m_bf[64 * k:64 * k + 64, 0:HALF].rearrange("p (i n) -> p i n", n=128),
                                   ACT.Copy).then_inc(comb_done, 1)
                act.wait_ge(m_full, M_LEN * b + M_AT["wo"] + 1)
                act.activation(r1[:, :], m_bank[:, :], ACT.Identity, bias=w("bo")).then_inc(r1_done, 1)

            def squares(n):
                act.wait_ge(xc_done, n + 1)
                act.activation(sq[:, :, :], xc[:, :, :], ACT.Square).then_inc(sq_done, 1)

            def turned_h1(b):
                act.wait_ge(m_full, M_LEN * b + M_AT["h1t"] + 1)
                for g in range(2):
                    act.activation(h1t[0:64, g * HALF:(g + 1) * HALF], m_bank[64 * g:64 * g + 64, :],
                                   ACT.Copy).then_inc(h1t_done, 1)

            def ffn(b):
                for kind, ch in FFN_STEPS:
                    n = R_AT[(kind, ch)]
                    act.wait_ge(r_full, R_LEN * b + n + 1)
                    bank = r_bank[n % 3]
                    if kind == "s1":
                        dst, src, bias = s1o[0:64, ch, :], bank[0:64, :], 0.0
                    elif kind[0] == "e":
                        dst, src, bias = e1o[:, ch, int(kind[1]), :], bank[:, :], 0.0
                    elif kind == "s2":
                        dst, src, bias = s2o[:, ch, :], bank[:, :], 0.0
                    else:
                        k = int(kind[1])
                        dst, src, bias = e2o[:, ch, k, :], bank[:, :], w("eb2")[:, k:k + 1]
                    if kind == "s1":
                        act.activation(logits[:, ch * HALF:(ch + 1) * HALF], bank[64:64 + E, :],
                                       ACT.Copy).then_inc(logits_done, 1)
                    act.activation(dst, src, ACT.Relu, bias=bias).then_inc(r_free, 1)
                    if (kind, ch) == ("e1", 0):
                        act.wait_ge(gd_done, 2 * b + 1)
                        act.activation(ge[:, :, :], gd[:, :, :], ACT.Exp).then_inc(ge_done, 1)
                    if (kind, ch) == ("e3", 0):
                        act.wait_ge(gd_done, 2 * b + 2)
                        act.activation(gu[:, :, :], gd[:, :, :], ACT.Exp).then_inc(gu_done, 1)
                    if (kind, ch) == FFN_STEPS[GATES_AT]:
                        act.wait_ge(m_full, M_LEN * b + M_AT["gt"] + 1)
                        act.activation(gwt[:, :], m_bank[0:E * NT, 0:128], ACT.Copy).then_inc(gwt_done, 1)
                n = R_AT[("l3",)]
                act.wait_ge(r_full, R_LEN * b + n + 1)
                act.activation(r2[:, :], r_bank[n % 3][:, :], ACT.Copy).then_inc(r_free, 1)

            def batch(b, last):
                exponentials(b)
                output(b)
                if not last:
                    raw_tokens(b + 1)
                squares(2 * b)
                if not last:
                    first_parts(b + 1)
                turned_h1(b)
                ffn(b)
                squares(2 * b + 1)

            act.wait_ge(packed, 16)
            raw_tokens(0)
            first_parts(0)
            with act.Fori(0, B - 1) as b:
                batch(b, False)
            batch(B - 1, True)

        @block.vector
        def _(dve):
            taken = [0, 0, 0]

            def step(ins):
                taken[1] += 1
                ins.then_inc(dve_step, 1)
                dve.wait_ge(dve_step, DVE_STEPS * taken[2] + (taken[0] + taken[1]))

            def setup():
                dve.memset(later[:, :, 0:1], 3.0).then_inc(sm_free, 2)
                dve.memset(later[:, :, 1:2], 2.0).then_inc(r_free, 3)
                dve.memset(later[:, :, 2:3], 1.0).then_inc(y_out, 1)
                step(dve.memset(later[:, :, 3:4], 0.0))
                dve.wait_ge(packed, 16)
                dve.tensor_copy(ident_bf[:, :], ident).then_inc(ident_set, 1)
                dve.wait_ge(mt_full, 1)
                for k in range(2):
                    src = ot_bank[k][0:64, :].rearrange("o (c k g j) -> o k j g c", k=2, g=2, j=4)
                    dst = mt[:, :].rearrange("o (k j g c) -> o k j g c", k=2, j=4, g=2)
                    for half in range(2):
                        dve.tensor_copy(dst[:, half, :, :, 32 * k:32 * k + 32], src[:, half]).then_inc(mt_read, 1)
                dve.wait_ge(wt_full, 1)
                dve.tensor_copy(wtok[:, :, :].rearrange("p k o -> p (k o)"), m_bank[:, :]).then_inc(wt_read, 1)
                dve.wait_ge(pool_set, 9)

            def clip(b):
                dve.wait_ge(raw_done, 2 * b + 2)
                for c, done in enumerate((sm_free, hc_done)):
                    s = slice(c * HALF, (c + 1) * HALF)
                    dve.tensor_scalar(hc[0:64, s], comb[64:128, s], CLIP, -CLIP, ALU.min, ALU.max).then_inc(done, 1)

            def rest_of(b, c):
                s = slice(c * HALF, (c + 1) * HALF)
                dve.wait_ge(p1_done, 2 * b + c + 1)
                dve.tensor_tensor(rest[:, s], ot_bank[c][:, :], parts[:, 0, s], ALU.subtract).then_inc(rest_done, 1)
                dve.wait_ge(rest_done, 2 * b + c + 1)
                dve.tensor_copy(parts[:, 1, s], rest[:, s]).then_inc(p2_done, 1)

            def values(b):
                dve.wait_ge(sm_full, SM_LEN * b + SM_AT[("v",)] + 1)
                dve.tensor_copy(vv[:, :, :, 0:DH].rearrange("p i h d -> p (i h) d"),
                                sm_bank[1][:, :].rearrange("p (i d) -> p i d", d=DH)).then_inc(sm_free, 1)

            def max_tile(b, h, m, c):
                n = SM_AT[("sm", h, m, c)]
                dve.wait_ge(sm_full, SM_LEN * b + n + 1)
                dve.tensor_reduce(mx2[:, h, m, c:c + 1], sm_bank[n % 2][:, :], AX.X, ALU.max).then_inc(sm_free, 1)
                if (m, c) == (NT - 1, 1):
                    dve.wait_ge(sm_free, SM_LEN * b + n + 3)
                    dve.tensor_reduce(ngm[:, h, :], mx2[:, h, :, :], AX.X, ALU.max, negate=True).then_inc(max_done, 1)

            def split_max(b, h):
                n = SM_AT[("t", h)]
                bank = sm_bank[n % 2][0:NT, 0:128]
                dve.wait_ge(sm_full, SM_LEN * b + n + 1)
                step(dve.tensor_copy(mpart[:, h % 2, 0, :], bank))
                dve.tensor_tensor(mrest[:, :], bank, mpart[:, h % 2, 0, :], ALU.subtract).then_inc(sm_free, 1)
                dve.wait_ge(sm_free, SM_LEN * b + n + 3)
                step(dve.tensor_copy(mpart[:, h % 2, 1, :], mrest[:, :]))
                dve.tensor_tensor(mpart[:, h % 2, 2, :], mrest[:, :], mpart[:, h % 2, 1, :],
                                  ALU.subtract).then_inc(mpart_done, 1)

            def maxima(b, keys):
                for key in keys:
                    if key[0] == "t":
                        split_max(b, key[1])
                    else:
                        max_tile(b, *key[1:])

            def head_out(b, h):
                dve.wait_ge(pv_done, H * NT * b + NT * (h + 1))
                dve.tensor_copy(osb[:, h, :], ot_bank[h % 2][:, 0:256]).then_inc(osb_done, 1)

            def divide(b, p):
                dve.wait_ge(m_full, M_LEN * b + M_AT[("t01", "t23")[p]] + 1)
                turned = m_bank[:, :].rearrange("p (k a j d) -> p k a j d", k=2, a=2, j=4)
                step(dve.reciprocal(rec[:, p, :, :].rearrange("p k n -> p (k n)"),
                                       m_bank[:, :].rearrange("p (n d) -> p n d", d=32)[:, :, DH]))
                for k in range(2):
                    h = 2 * p + k
                    dst = ao[:, :, DH * h:DH * h + DH].rearrange("p (j a) d -> p a j d", a=2)
                    dve.tensor_tensor(dst, turned[:, k, :, :, 0:DH],
                                      rec[:, p, k, :].rearrange("p (a j) -> p a j", a=2).unsqueeze(3)
                                      .to_broadcast([128, 2, 4, DH]), ALU.mult).then_inc(ao_done, 1)

            def spread(v):
                return v.unsqueeze(2).to_broadcast([128, NT, D])

            def centre(b, n, key):
                dve.wait_ge(m_full, M_LEN * b + M_AT[key] + 1)
                r = m_bank[:, :].rearrange("p (g o) -> p g o", o=D)
                step(dve.tensor_reduce(st[:, 0, :], r, AX.X, ALU.add))
                step(dve.tensor_scalar(st[:, 1, :], st[:, 0, :], -1.0 / D, None, ALU.mult))
                dve.tensor_tensor(xc[:, :, :], r, spread(st[:, 1, :]), ALU.add).then_inc(xc_done, 1)

            def variance(b, n):
                dve.wait_ge(sq_done, n + 1)
                step(dve.tensor_reduce(st[:, 2, :], sq[:, :, :], AX.X, ALU.add))
                dve.tensor_scalar(st[:, 3, :], st[:, 2, :], 1.0 / D, EPS, ALU.mult, ALU.add).then_inc(var_done, 1)

            def first_norm(b):
                dve.wait_ge(rstd_done, 2 * b + 1)
                dve.tensor_tensor(h1[:, :, :], xc[:, :, :], spread(st[:, 4, :]), ALU.mult).then_inc(h1_done, 1)

            def second_norm(b):
                dve.wait_ge(rstd_done, 2 * b + 2)
                dve.wait_ge(y_out, 32 * b + 1)
                dve.tensor_tensor(y[:, :, :].rearrange("p (a c) o -> p c a o", a=2),
                                  xc[:, :, :].rearrange("p (c a) o -> p c a o", a=2),
                                  st[:, 4, :].rearrange("p (c a) -> p c a", a=2).unsqueeze(3)
                                  .to_broadcast([128, 4, 2, D]), ALU.mult).then_inc(y_done, 1)

            def gates(b):
                def over(v):
                    return v.unsqueeze(2).to_broadcast([128, NT, E])

                dve.wait_ge(m_full, M_LEN * b + M_AT["gl"] + 1)
                dve.tensor_copy(gl[:, :, :].rearrange("p i e -> p (i e)"), m_bank[:, 0:NT * E]).then_inc(gl_done, 1)
                dve.wait_ge(gl_done, b + 1)
                step(dve.tensor_reduce(gs[:, 0, :], gl[:, :, :], AX.X, ALU.max))
                dve.tensor_tensor(gd[:, :, :], gl[:, :, :], over(gs[:, 0, :]), ALU.subtract).then_inc(gd_done, 1)
                dve.wait_ge(ge_done, b + 1)
                step(dve.tensor_reduce(gs[:, 1, :], ge[:, :, :], AX.X, ALU.add))
                step(dve.reciprocal(gs[:, 2, :], gs[:, 1, :]))
                step(dve.tensor_tensor(gp[:, :, :], ge[:, :, :], over(gs[:, 2, :]), ALU.mult))
                step(dve.tensor_reduce(gs[:, 3, :], gp[:, :, :], AX.X, ALU.max))
                dve.tensor_tensor(gd[:, :, :], gp[:, :, :], over(gs[:, 3, :]), ALU.subtract).then_inc(gd_done, 1)
                for k in range(1, E):
                    ins = dve.tensor_tensor(gc[:, k, :, 0:E - k], gp[:, :, 0:E - k], gp[:, :, k:E], ALU.is_ge)
                    step(ins)
                before = later
                for k in range(1, E):
                    if k == 1:
                        step(dve.tensor_tensor(rank[:, :, 0:E - 1], later[:, :, 0:E - 1], gc[:, 1, :, 0:E - 1],
                                                  ALU.subtract))
                        step(dve.tensor_copy(rank[:, :, E - 1:E], later[:, :, E - 1:E]))
                    else:
                        step(dve.tensor_tensor(rank[:, :, 0:E - k], rank[:, :, 0:E - k], gc[:, k, :, 0:E - k],
                                                  ALU.subtract))
                    step(dve.tensor_tensor(rank[:, :, k:E], rank[:, :, k:E], gc[:, k, :, 0:E - k], ALU.add))
                dve.wait_ge(gu_done, b + 1)
                step(dve.scalar_tensor_tensor(out=gm[:, :, :], in0=rank[:, :, :], scalar=2.0, in1=gu[:, :, :],
                                                 op0=ALU.is_lt, op1=ALU.mult))
                step(dve.tensor_reduce(gs[:, 4, :], gm[:, :, :], AX.X, ALU.add))
                step(dve.reciprocal(gs[:, 5, :], gs[:, 4, :]))
                dve.tensor_tensor(gw[:, :, :].rearrange("p e i -> p i e"), gm[:, :, :], over(gs[:, 5, :]),
                                  ALU.mult).then_inc(gw_done, 1)

            def weigh_experts(b, ch):
                if ch == 0:
                    dve.wait_ge(gate_in, 80 * (b + 1))
                for k in range(2):
                    dve.wait_ge(r_free, R_LEN * b + R_AT[(f"p{k}", ch)] + 4)
                    dve.tensor_tensor(e2g[:, ch, k, :], e2o[:, ch, k, :], wgb[:, k, ch * HALF:(ch + 1) * HALF],
                                      ALU.mult).then_inc(e2g_done, 1)

            def batch(b, last):
                taken[:] = taken[0] + taken[1], 0, b
                for h in range(H):
                    for m in range(NT):
                        maxima(b, BESIDE.get((h, m), ()))
                        if h > 0 and m == 2:
                            head_out(b, h - 1)
                    if h == 2:
                        divide(b, 0)
                head_out(b, H - 1)
                divide(b, 1)
                if not last:
                    clip(b + 1)
                centre(b, 2 * b, "r1t")
                if not last:
                    rest_of(b + 1, 0)
                variance(b, 2 * b)
                if not last:
                    rest_of(b + 1, 1)
                    values(b + 1)
                first_norm(b)
                gates(b)
                if not last:
                    for n in range(AHEAD0, len(FFN_STEPS)):
                        maxima(b + 1, FIRST_MAX[slice(*AHEAD[n])])
                        if n == 13:
                            weigh_experts(b, 0)
                    maxima(b + 1, FIRST_MAX[19:20])
                    weigh_experts(b, 1)
                    maxima(b + 1, FIRST_MAX[20:22])
                else:
                    weigh_experts(b, 0)
                    weigh_experts(b, 1)
                centre(b, 2 * b + 1, "r2t")
                if not last:
                    maxima(b + 1, FIRST_MAX[22:24])
                variance(b, 2 * b + 1)
                if not last:
                    maxima(b + 1, FIRST_MAX[24:])
                second_norm(b)
                assert last or taken[1] == DVE_STEPS, taken[1]

            setup()
            clip(0)
            rest_of(0, 0)
            rest_of(0, 1)
            values(0)
            maxima(0, FIRST_MAX)
            with dve.Fori(0, B - 1) as b:
                batch(b, False)
            taken[0] -= DVE_STEPS
            batch(B - 1, True)


def packed_weights(a):
    import numpy as np

    pack = np.zeros((128, PACK_COLS), np.float32)

    def put(name, value, r0=0, c0=0):
        value = np.asarray(value)
        at = PACK[name][1]
        pack[r0:r0 + value.shape[0], at + c0:at + c0 + value.shape[1]] = value

    by_dim = np.arange(D).reshape(H, DH).T.reshape(-1)
    put("ident", np.eye(128))
    for n, k in enumerate("qk"):
        put("wqk", a[f"L0_attn_W{k}"][by_dim].T, 0, D * n)
        put("wqk", a[f"L0_attn_b{k}"][by_dim][None], D, D * n)
    put("wv", a["L0_attn_Wv"].T)
    put("wv", a["L0_attn_bv"][None], D)
    put("wo", a["L0_attn_Wo"].T)
    put("wo", np.eye(D), D)
    put("bo", a["L0_attn_bo"][:, None])
    put("bo", a["L0_attn_bo"][:, None], D)
    put("s1", a["L0_ffn_sW1"])
    put("s1", a["L0_ffn_sb1"][None], D)
    put("s1", a["L0_ffn_gW"], 0, D)
    put("s1", a["L0_ffn_gb"][None], D, D)
    put("s2", a["L0_ffn_sW2"])
    put("s2", a["L0_ffn_sb2"][None], D)
    put("s3", a["L0_ffn_sW3"])
    put("w3", np.eye(D))
    put("w3", a["L0_ffn_sb3"][None], D)
    put("w3", a["L0_ffn_eb3"], KW)
    for e in range(E):
        put("e1", a["L0_ffn_eW1"][e], 0, 128 * e)
        put("e1", a["L0_ffn_eb1"][e][None], D, 128 * e)
        put("e2", a["L0_ffn_eW2"][e], 0, 64 * e)
        put("eb2", a["L0_ffn_eb2"][e][:, None], 64 * (e % 2), e // 2)
        put("e3", a["L0_ffn_eW3"][e], 64 * (e % 2), 64 * (e // 2))
    angle = 2 * np.pi * np.arange(RF // 2)[:, None] * np.arange(PATCH)[None] / PATCH
    dft = np.concatenate([np.cos(angle), -np.sin(angle)]) / np.sqrt(PATCH)
    dft[np.abs(dft) < 1e-12] = 0.0
    tok = a["L0_tok_W"].reshape(D, RF, C // CG, CG)
    for c in range(CG):
        put("dft", dft, RF * c, PATCH * c)
        put("wt", tok[:, :, :, c].transpose(1, 2, 0).reshape(RF, -1), RF * c)
    return pack


def kernel(**inputs):
    import numpy as np
    import concourse.bacc as bacc
    from concourse.bass_utils import run_bass_kernel_spmd

    a = {k: np.asarray(v) for k, v in inputs.items()}
    arrays = {"x": np.ascontiguousarray(a["x"]), "pack": packed_weights(a)}
    nc = bacc.Bacc("TRN2", target_bir_lowering=False, num_devices=1)
    args = [nc.dram_tensor(n, v.shape, mybir.dt.from_np(v.dtype), kind="ExternalInput").ap() for n, v in arrays.items()]
    out = nc.dram_tensor("out", (B, N, D), F32, kind="ExternalOutput").ap()
    vit_layer(nc, *args, out)
    r = run_bass_kernel_spmd(nc, [arrays], core_ids=[0])
    return r.results[0]["out"]
```

```python
from contextlib import ExitStack

import concourse.bass as bass
from concourse import mybir

F32 = mybir.dt.float32
BF16 = mybir.dt.bfloat16
ALU = mybir.AluOpType
ACT = mybir.ActivationFunctionType
AX = mybir.AxisListType

B, C, T, V = 4, 64, 128, 64
PATCH, STRIDE, NPATCH = 16, 8, 16
RF = PATCH + 2
CG = 4
N = V * NPATCH
D, H, DH = 64, 4, 16
NT = N // 128
HALF = N // 2
E = 4
SCALE = float(DH) ** -0.5
CLIP = 10000.0
EPS = 1e-5
TERMS_Q = (0, 1, 2, 0, 1, 0)
TERMS_K = (2, 1, 0, 1, 0, 0)
RUNS = ((0, 3), (3, 5), (5, 6))
KS = 16 * len(TERMS_Q)
KM = KS + 3
KW = 96

PACK, _at = {}, 0
for _name, _rows, _cols in (
    ("ident", 128, 128), ("dft", KW, CG * PATCH), ("wt", KW, 16 * 64), ("wqk", KW, 128), ("wv", KW, 64), ("wo", 128, 64), ("bo", 128, 1),
    ("s1", KW, 64 + E), ("e1", KW, 128 * E), ("s2", KW, 128), ("e2", 128, 64 * E), ("eb2", 128, 2),
    ("w3", KW + E, 64), ("s3", 128, 64), ("e3", 128, 128),
):
    PACK[_name] = (_rows, _at, _cols)
    _at += _cols
PACK_COLS = _at
TOKEN_COLS = PACK["wqk"][1]

STAGES = H * NT
T23_AT, TURN_OUTPUT_AT, OUTPUT_AT, R1T_AT, VAR1_AT, NORM1_AT, H1T_AT = 3, 4, 5, 6, 7, 8, 9
TOKEN_STAGES = (5, 5, 6, 6, 7, 7, 9, 9)
CLIP_AT, QK_AT, LOGITS_AT, V_AT = 9, 10, 11, 12
SHARE_AT, RANK_AT, CHOOSE_AT, GATES_AT = 12, 13, 14, 15
WEIGH_AT = {19: 0, 25: 1}
LAST_AT, R2T_AT, T01_AT, VAR2_AT, NORM2_AT = 25, 27, 28, 28, 29
FFN_STEPS = [("s1", 0), ("s1", 1)] + [(k, ch) for ch in range(2) for k in ("e0", "e1", "e2", "e3", "s2", "p0", "p1")]
STEP_STAGES = (10, 10, 11, 13, 13, 13, 15, 16, 17, 18, 18, 19, 20, 21, 22, 23)
FFN_AT = {_s: [k for k, at in zip(FFN_STEPS, STEP_STAGES) if at == _s] for _s in range(STAGES)}
assert FFN_AT[LOGITS_AT]

AHEAD1 = 8
def _head_tiles(who, h):
    return [(who, "sm", h, m, c) for m in range(NT) for c in range(2)]


_n0, _n1 = _head_tiles("n", 0), _head_tiles("n", 1)[:AHEAD1]
NEXT_MAX = _n0[2:] + _n1[:2] + [("n", "t", 0)] + _n1[2:]
_line = _head_tiles("a", 1)[AHEAD1:]
for _h in (2, 3):
    _line += _head_tiles("a", _h)[:2] + [("a", "t", _h - 1)] + _head_tiles("a", _h)[2:]
_line += _n0[:2] + [("a", "t", 3)] + NEXT_MAX
FIRST_MAX = _n0[:2] + NEXT_MAX
COUNTS = (2, 3, 3, 2, 2, 4, 1, 3, 2, 0, 3, 3, 0, 1, 2, 2, 3, 3, 2, 3, 1, 2, 3, 3, 2, 2, 2, 2, 2, 2, 1, 2)
BESIDE = {}
for _s in range(STAGES):
    BESIDE[_s], _line = _line[:COUNTS[_s]], _line[COUNTS[_s]:]
assert not _line

SM_SEQ, R_SEQ = [], []
for _s in range(STAGES):
    SM_SEQ += BESIDE[_s] + ([("n", "qk", 0), ("n", "qk", 1)] if _s == QK_AT else [])
    R_SEQ += [("a", "st", _s, c) for c in range(2)] + [("p", *k) for k in FFN_AT.get(_s, ())]
    R_SEQ += [("p", "l3")] if _s == LAST_AT else []
_of_stage = (("p", "t23", T23_AT), ("p", "aot", TURN_OUTPUT_AT), ("p", "wo", OUTPUT_AT), ("p", "r1t", R1T_AT),
             ("p", "h1t", H1T_AT), ("p", "gt", GATES_AT), ("p", "r2t", R2T_AT), ("p", "gl", LOGITS_AT),
             ("a", "t01", T01_AT))
M_SEQ = [e[:2] for e in sorted(_of_stage, key=lambda e: e[2])]
PROLOGUE = {"sm": [("n", "qk", 0), ("n", "qk", 1)] + FIRST_MAX, "r": [], "m": []}
SEQ = {"sm": SM_SEQ, "r": R_SEQ, "m": M_SEQ}
assert len(SM_SEQ) % 2 == 0 and len(R_SEQ) % 3 == 0


class Turn:

    def __init__(self, p, a, n, kind):
        self.p, self.a, self.n, self.kind = p, a, n, kind
        have = [k for k, v in (("p", p), ("a", a), ("n", n)) if v is not None]
        self.seq = PROLOGUE if kind == "prologue" else {r: [e for e in q if e[0] in have] for r, q in SEQ.items()}
        self.start = {}
        for r, q in SEQ.items():
            first = len(PROLOGUE[r])
            second = first + len([e for e in q if e[0] != "p"])
            last = second + (B - 2) * len(q)
            after = last + len([e for e in q if e[0] != "n"])
            self.start[r] = {"prologue": 0, "first": first, "loop": second, "last": last, "epilogue": after}[kind]

    def bank(self, ring, key, banks):
        return (self.start[ring] + self.seq[ring].index(key)) % banks

    def uses(self, ring, key=None):
        n = self.start[ring] + (self.seq[ring].index(key) if key else 0)
        return n + len(SEQ[ring]) * self.p if self.kind == "loop" else n


def run_turns(engine, turn):
    turn(FIRST_TURN)
    with engine.Fori(0, B - 2) as b:
        turn(Turn(b, b + 1, b + 2, "loop"))
    turn(Turn(B - 2, B - 1, None, "last"))
    turn(Turn(B - 1, None, None, "epilogue"))


PROLOGUE_TURN = Turn(None, None, 0, "prologue")
FIRST_TURN = Turn(None, 0, 1, "first")
DVE_STEPS = 32
NPT = 4


def vit_layer(nc, x, pack, out):
    with ExitStack() as ctx:
        def sb(name, shape, dt=F32):
            return ctx.enter_context(nc.sbuf_tensor(name, shape, dt))

        def sem(name):
            return ctx.enter_context(nc.semaphore(name))

        banks = [ctx.enter_context(nc.psum_tensor(f"bank{i}", [128, 512], F32)) for i in range(8)]
        sm_bank, r_bank, ot_bank, token_bank, m_bank = banks[0:2], banks[2:5], banks[5], banks[6], banks[7]
        m_bf = m_bank[:, :].bitcast(BF16)

        qk_dram = nc.dram_tensor("qk_dram", (2, 3 * DH, H * N), BF16)
        mx_dram = nc.dram_tensor("mx_dram", (H, NT, 3, 128), BF16)
        gate_dram = nc.dram_tensor("gate_dram", (E, N), F32)

        pk = sb("pk", [128, PACK_COLS])

        def w(name, r0=0, r1=None):
            rows, at, cols = PACK[name]
            return pk[r0:rows if r1 is None else r1, at:at + cols]

        ident = w("ident")
        ident_bf = sb("ident_bf", [128, 128], BF16)
        mt = sb("mt", [64, CG * 16 * PATCH])
        wtok = sb("wtok", [128, 8, 64])
        xs = sb("xs", [128, NPATCH + 1, 4 * V])
        raw = sb("raw", [128, N])
        vst = sb("vst", [128, NT, D])
        comb = sb("comb", [128, N])
        hc = sb("hc", [KW, N])
        vv = sb("vv", [128, NT, H, 32])
        parts = sb("parts", [128, 3, N], BF16)
        rest = sb("rest", [128, N])
        qst = sb("qst", [KM, H, N], BF16)
        kst = sb("kst", [KM, H, N], BF16)
        pt = sb("pt", [128, NPT, N])
        mx2 = sb("mx2", [128, H, NT, 2])
        ngm = sb("ngm", [128, H, NT])
        mrest = sb("mrest", [NT, 128])
        mpart = sb("mpart", [NT, 2, 3, 128], BF16)
        osb = sb("osb", [128, H, 256])
        rec = sb("rec", [128, 2, 2, 8])
        ao = sb("ao", [128, NT, D], BF16)
        r1 = sb("r1", [128, HALF])
        r2 = sb("r2", [128, HALF])
        xc = sb("xc", [128, NT, D])
        sq = sb("sq", [128, NT, D])
        st = sb("st", [128, 5, NT])
        halfpow = sb("halfpow", [128, NT])
        zero = sb("zero", [128, NT * H])
        h1 = sb("h1", [128, NT, D])
        h1t = sb("h1t", [KW + E, N])
        y = sb("y", [128, NT, D])
        s1o = sb("s1o", [KW, 2, HALF])
        logits = sb("logits", [E, N])
        s2o = sb("s2o", [128, 2, HALF])
        e1o = sb("e1o", [128, 2, E, HALF])
        e2o = sb("e2o", [128, 2, 2, HALF])
        e2g = sb("e2g", [128, 2, 2, HALF])
        wgb = sb("wgb", [128, 2, N])
        gl = sb("gl", [128, NT, E])
        gd = sb("gd", [128, NT, E])
        ge = sb("ge", [128, NT, E])
        gp = sb("gp", [128, NT, E])
        gu = sb("gu", [128, NT, E])
        later = sb("later", [128, NT, E])
        rank = sb("rank", [128, NT, E])
        gm = sb("gm", [128, NT, E])
        gc = sb("gc", [128, E, NT, E])
        gs = sb("gs", [128, 6, NT])
        gw = sb("gw", [128, E, NT])
        gwt = sb("gwt", [E * NT, 128])

        token_packed = sem("token_packed")
        packed, x_in, stack01_in, stack23_in, mrow_out, mrow_in = (
            sem(n) for n in ("packed", "x_in", "stack01_in", "stack23_in", "mrow_out", "mrow_in"))
        parts_out, gate_out, gate_in, y_out = (sem(n) for n in ("parts_out", "gate_out", "gate_in", "y_out"))
        ones_set, ident_set, mt_full, mt_read, wt_full, wt_read, pool_set = (
            sem(n) for n in ("ones_set", "ident_set", "mt_full", "mt_read", "wt_full", "wt_read", "pool_set"))
        sm_full, sm_free, r_full, r_free, m_full = (sem(n) for n in ("sm_full", "sm_free", "r_full", "r_free", "m_full"))
        res_done, p1_done, rest_done, p2_done, p3_done = (
            sem(n) for n in ("res_done", "p1_done", "rest_done", "p2_done", "p3_done"))
        raw_done, hc_done, pv_done, osb_done, ao_done = (
            sem(n) for n in ("raw_done", "hc_done", "pv_done", "osb_done", "ao_done"))
        max_done, mpart_done, comb_done, r1_done = (sem(n) for n in ("max_done", "mpart_done", "comb_done", "r1_done"))
        xc_done, sq_done, var_done, rstd_done, h1_done, h1t_done, y_done = (
            sem(n) for n in ("xc_done", "sq_done", "var_done", "rstd_done", "h1_done", "h1t_done", "y_done"))
        token_full = sem("token_full")
        logits_done, val_done, vv_done = (sem(n) for n in ("logits_done", "val_done", "vv_done"))
        gl_done, gd_done, ge_done, gu_done, gw_done, gwt_done, e2g_done = (
            sem(n) for n in ("gl_done", "gd_done", "ge_done", "gu_done", "gw_done", "gwt_done", "e2g_done"))
        dve_step = sem("dve_step")

        block = ctx.enter_context(nc.Block())

        x_v = x.rearrange("b c (n g j) v -> b g c n (j v)", n=NPATCH, g=2, j=4)
        x_last = x[:, :, T - 1, :]
        out_v = out.rearrange("b (v g i) o -> b g v (i o)", v=V, g=2, i=NT)

        def token_weight_halves(k, half):
            src = (ot_bank, token_bank)[k][0:64, :].rearrange("o (c k g j) -> o k j g c", k=2, g=2, j=4)
            dst = mt[:, :].rearrange("o (k j g c) -> o k j g c", k=2, j=4, g=2)
            return dst[:, half, :, :, 32 * k:32 * k + 32], src[:, half]

        @block.sync
        def _(sp):
            def load_x(b):
                for g in range(2):
                    sp.dma_start(xs[64 * g:64 * g + 64, 0:NPATCH, :], x_v[b, g]).then_inc(x_in, 16)
                    sp.dma_start(xs[64 * g:64 * g + 64, NPATCH, :].rearrange("p (j v) -> p j v", j=4),
                                 x_last[b].unsqueeze(1).to_broadcast([64, 4, V])).then_inc(x_in, 16)

            def parts_to_dram(b, first=False):
                if not first:
                    sp.wait_ge(stack23_in, 96 * b)
                for part, done in enumerate((p1_done, p2_done, p3_done)):
                    sp.wait_ge(done, 2 * b + 2)
                    for side in range(2):
                        place = (2 - part if side else part) * DH
                        sp.dma_start(qk_dram[side, place:place + DH, :].rearrange("d (h n) -> (d h) n", h=H),
                                     parts[64 * side:64 * side + 64, part, :]).then_inc(parts_out, 16)

            def stacks(b, h0):
                sp.wait_ge(parts_out, 96 * (b + 1))
                for side, dst in enumerate((qst, kst)):
                    for t0, t1 in RUNS:
                        r0 = DH * (2 - TERMS_K[t0] if side else TERMS_Q[t0])
                        arrived = stack23_in if h0 else stack01_in
                        sp.dma_start(dst[DH * t0:DH * t1, h0:h0 + 2, :].rearrange("p h n -> p (h n)"),
                                     qk_dram[side, r0:r0 + DH * (t1 - t0), N * h0:N * h0 + 2 * N]).then_inc(arrived, 16)

            def max_rows(b, h):
                sp.wait_ge(mpart_done, H * b + h + 1)
                sp.dma_start(mx_dram[h], mpart[:, h % 2, :, :]).then_inc(mrow_out, 16)
                sp.wait_ge(mrow_out, 16 * (H * b + h + 1))
                sp.dma_start(qst[KS:KM, h, :].rearrange("p (j n) -> p j n", j=NT),
                             mx_dram[h].rearrange("j t n -> t j n")).then_inc(mrow_in, 16)

            def gates(b):
                sp.wait_ge(gwt_done, b + 1)
                sp.dma_start(gate_dram.ap().rearrange("e (i n) -> (e i) n", i=NT), gwt[:, :]).then_inc(gate_out, 16)
                sp.wait_ge(gate_out, 16 * (b + 1))
                for e in range(E):
                    sp.dma_start(wgb[64 * (e % 2):64 * (e % 2) + 64, e // 2, :],
                                 gate_dram[e:e + 1, :].to_broadcast([64, N])).then_inc(gate_in, 16)
                sp.dma_start(h1t[KW:KW + E, :], gate_dram.ap()).then_inc(gate_in, 16)

            def store(b):
                sp.wait_ge(y_done, b + 1)
                for g in range(2):
                    sp.dma_start(out_v[b, g], y[64 * g:64 * g + 64, :, :].rearrange("p i o -> p (i o)")).then_inc(y_out, 16)

            def turn(t):
                p, a, n = t.p, t.a, t.n
                if p is not None and a is not None:
                    sp.wait_ge(r_full, t.uses("r"))
                    stacks(a, 2)
                if n is not None and t is not FIRST_TURN:
                    sp.wait_ge(raw_done, 2 * a + 2)
                    load_x(n)
                if a is not None:
                    max_rows(a, 1)
                if n is not None:
                    parts_to_dram(n)
                if a is not None:
                    max_rows(a, 2)
                if p is not None:
                    gates(p)
                if n is not None:
                    sp.wait_ge(r_full, t.uses("r", ("a", "st", 2 * NT - 1, 1)) + 1)
                    stacks(n, 0)
                if a is not None:
                    max_rows(a, 3)
                if n is not None:
                    max_rows(n, 0)
                if p is not None:
                    store(p)

            sp.dma_start(pk[:, 0:TOKEN_COLS], pack[:, 0:TOKEN_COLS]).then_inc(token_packed, 16)
            load_x(0)
            sp.dma_start(pk[:, TOKEN_COLS:], pack[:, TOKEN_COLS:]).then_inc(packed, 16)
            sp.wait_ge(raw_done, 2)
            load_x(1)
            parts_to_dram(0, first=True)
            stacks(0, 0)
            stacks(0, 2)
            max_rows(0, 0)
            run_turns(sp, turn)
            sp.wait_ge(y_out, 32 * B + 1)

        @block.gpsimd
        def _(pool):
            for n, (dst, value) in enumerate((
                    (hc[64:KW, :], 0.0), (h1t[64:KW, :], 0.0), (s1o[64:KW, :, :], 0.0),
                    (hc[64:65, :], 1.0), (h1t[64:65, :], 1.0), (s1o[64:65, :, :], 1.0), (vv[:, :, :, 16:32], 1.0),
                    (kst[KS:KM, :, :], 1.0), (halfpow[:, :], -0.5))):
                if n:
                    pool.wait_ge(pool_set, n)
                pool.memset(dst, value).then_inc(pool_set, 1)
            pool.wait_ge(pool_set, 9)
            pool.memset(zero[:, :], 0.0).then_inc(rstd_done, 1)
            pool.wait_ge(rstd_done, 1)

            def third_parts(b, first=False):
                if not first:
                    pool.wait_ge(res_done, b)
                for c in range(2):
                    s = slice(c * HALF, (c + 1) * HALF)
                    pool.wait_ge(p2_done, 2 * b + c + 1)
                    pool.tensor_tensor(parts[:, 2, s], rest[:, s], parts[:, 1, s], ALU.subtract).then_inc(p3_done, 1)

            def rstd(n):
                pool.wait_ge(var_done, n + 1)
                pool.tensor_tensor(st[:, 4, :], st[:, 3, :], halfpow[:, :], ALU.pow).then_inc(rstd_done, 1)

            def turn(t):
                p, a, n = t.p, t.a, t.n
                if a is not None:
                    if p is not None:
                        pool.wait_ge(rstd_done, 2 * p + 1)
                        pool.wait_ge(pv_done, H * NT * a)
                    pool.wait_ge(val_done, a + 1)
                    kept = vst[:, :, :].rearrange("p i (h d) -> p (i h) d", d=DH)
                    pool.tensor_tensor(vv[:, :, :, 0:DH].rearrange("p i h d -> p (i h) d"), kept,
                                       zero[:, :].unsqueeze(2).to_broadcast([128, NT * H, DH]),
                                       ALU.subtract).then_inc(vv_done, 1)
                    if p is not None:
                        pool.wait_ge(m_full, t.uses("m", ("p", "wo")) + 1)
                    pool.wait_ge(raw_done, 2 * a + 2)
                    pool.wait_ge(vv_done, a + 1)
                    pool.tensor_tensor(comb[64:128, :], raw[64:128, :], zero[64:128, 0:1].to_broadcast([64, N]),
                                       ALU.subtract).then_inc(res_done, 1)
                if p is not None:
                    if a is not None:
                        pool.wait_ge(res_done, a + 1)
                    rstd(2 * p)
                if n is not None:
                    if p is not None:
                        pool.wait_ge(rstd_done, 2 * p + 2)
                    third_parts(n)
                if p is not None:
                    pool.wait_ge(rstd_done, 2 * p + 2)
                    if n is not None:
                        pool.wait_ge(p3_done, 2 * n + 2)
                    rstd(2 * p + 1)

            third_parts(0, first=True)
            run_turns(pool, turn)

        @block.tensor
        def _(pe):
            def sm_slot(t, key):
                pe.wait_ge(sm_free, t.uses("sm", key) + 1)
                return sm_bank[t.bank("sm", key, 2)]

            def r_slot(t, key):
                pe.wait_ge(r_free, t.uses("r", key) + 1)
                return r_bank[t.bank("r", key, 3)]

            m_read = {"t01": (ao_done, 4, 2), "t23": (ao_done, 4, 4), "aot": (comb_done, 2, 2), "wo": (r1_done, 1, 1),
                      "r1t": (xc_done, 2, 1), "h1t": (h1t_done, 2, 2), "gl": (gl_done, 1, 1), "gt": (gwt_done, 1, 1),
                      "r2t": (xc_done, 2, 2)}

            def m_slot(t, key):
                at = t.seq["m"].index(key)
                if at:
                    who, name = t.seq["m"][at - 1]
                    x = {"p": t.p, "a": t.a, "n": t.n}[who]
                elif t.kind == "first":
                    return
                else:
                    name, x = "t01", t.p
                done, per, offset = m_read[name]
                pe.wait_ge(done, per * x + offset)

            def setup():
                pe.wait_ge(token_packed, 16)
                for g in range(16):
                    mm = pe.matmul((ot_bank, token_bank)[g // 8][0:64, 64 * (g % 8):64 * (g % 8) + 64],
                                   w("wt")[:, 64 * g:64 * g + 64], w("dft"), start=True, stop=True)
                mm.then_inc(mt_full, 1)
                pe.wait_ge(mt_read, 4)
                for kt in range(8):
                    mm = pe.transpose(m_bank[:, 64 * kt:64 * kt + 64], mt[:, 128 * kt:128 * kt + 128], ident[0:64, 0:64])
                mm.then_inc(wt_full, 1)
                pe.wait_ge(wt_read, 1)
                pe.wait_ge(ident_set, 1)
                pe.wait_ge(pool_set, 9)

            def tokens(t, k0=0, k1=8):
                if k0 == 0:
                    if t.a is not None:
                        pe.wait_ge(val_done, t.n)
                    pe.wait_ge(x_in, 64 * (t.n + 1))
                for kt in range(k0, k1):
                    for nn in range(2):
                        n0 = 8 * nn + kt // 4
                        mm = pe.matmul(token_bank[64 * nn:64 * nn + 64, :], wtok[:, kt, :],
                                       xs[:, n0:n0 + 8, V * (kt % 4):V * (kt % 4) + V],
                                       start=(kt == 0), stop=(kt == 7))
                if k1 == 8:
                    mm.then_inc(token_full, 1)

            def project_qk(t):
                pe.wait_ge(hc_done, 2 * t.n + 2)
                for c in range(2):
                    bank = sm_slot(t, ("n", "qk", c))
                    pe.matmul(bank[:, :], w("wqk"), hc[:, c * HALF:(c + 1) * HALF],
                              start=True, stop=True).then_inc(sm_full, 1)

            def project_v(t):
                pe.wait_ge(raw_done, 2 * t.n + 2)
                for i in range(NT):
                    mm = pe.matmul(token_bank[:, D * i:D * i + D], hc[:, 128 * i:128 * i + 128], w("wv"),
                                   start=True, stop=True)
                mm.then_inc(token_full, 1)

            def maxima(t, keys):
                for key in keys:
                    if key not in t.seq["sm"]:
                        continue
                    x = t.n if key[0] == "n" else t.a
                    bank = sm_slot(t, key)
                    if key[1] == "t":
                        pe.wait_ge(max_done, H * x + key[2] + 1)
                        pe.transpose(bank[0:NT, 0:128], ngm[:, key[2], :], ident).then_inc(sm_full, 1)
                        continue
                    h, m, c = key[2:]
                    if (h, m, c) == (0, 0, 0):
                        pe.wait_ge(stack01_in, 96 * (x + 1))
                    if (h, m, c) == (2, 0, 0):
                        pe.wait_ge(stack23_in, 96 * (x + 1))
                    pe.matmul(bank[:, :], qst[0:KS, h, 128 * m:128 * m + 128], kst[0:KS, h, c * HALF:(c + 1) * HALF],
                              start=True, stop=True).then_inc(sm_full, 1)

            def scores(t, s):
                h, m = s // NT, s % NT
                if m == 0:
                    pe.wait_ge(mrow_in, 16 * (H * t.a + h + 1))
                for c in range(2):
                    bank = r_slot(t, ("a", "st", s, c))
                    pe.matmul(bank[:, :], kst[0:KM, h, 128 * m:128 * m + 128], qst[0:KM, h, c * HALF:(c + 1) * HALF],
                              start=True, stop=True).then_inc(r_full, 1)

            def weigh(t, b, h, m):
                if b is t.p:
                    pe.wait_ge(r_free, t.uses("r") - 2 * (NT - 1 - m) + 3)
                else:
                    pe.wait_ge(r_free, t.uses("r", ("a", "st", NT * h + m, 1)) + 4)
                if m == 0:
                    if t.p is not None or h > 0:
                        pe.wait_ge(osb_done, H * b + h)
                    if h == 0:
                        pe.wait_ge(vv_done, b + 1)
                for j in range(4):
                    mm = pe.matmul(ot_bank[32 * j:32 * j + 32, 0:256], vv[:, m, h, :],
                                   pt[:, m % NPT, 256 * j:256 * j + 256], start=(m == 0), stop=(m == NT - 1),
                                   tile_position=(0, 32 * j))
                mm.then_inc(pv_done, 1)

            def turn_heads(t, who, pair):
                b = t.p if who == "p" else t.a
                m_slot(t, (who, ("t01", "t23")[pair]))
                pe.wait_ge(osb_done, H * b + 2 * pair + 2)
                for n in range(4):
                    mm = pe.transpose(m_bank[:, 128 * n:128 * n + 128],
                                      osb[:, 2 * pair + n // 2, 128 * (n % 2):128 * (n % 2) + 128], ident)
                mm.then_inc(m_full, 1)

            def turn_output(t):
                m_slot(t, ("p", "aot"))
                pe.wait_ge(ao_done, 4 * t.p + 4)
                for i in range(NT // 2):
                    mm = pe.transpose(m_bf[:, 128 * i:128 * i + 128],
                                      ao[:, 2 * i:2 * i + 2, :].rearrange("p a o -> p (a o)"), ident_bf[:, :])
                mm.then_inc(m_full, 1)

            def output(t):
                m_slot(t, ("p", "wo"))
                pe.wait_ge(res_done, t.p + 1)
                for c in range(2):
                    mm = pe.matmul(m_bank[64 * c:64 * c + 64, :], w("wo"), comb[:, c * HALF:(c + 1) * HALF],
                                   start=True, stop=True)
                mm.then_inc(m_full, 1)

            def turn_residual(t, name, src):
                m_slot(t, ("p", name))
                if name == "r1t":
                    pe.wait_ge(r1_done, t.p + 1)
                else:
                    pe.wait_ge(r_free, t.uses("r", ("p", "l3")) + 4)
                for c in range(4):
                    mm = pe.transpose(m_bank[:, 128 * c:128 * c + 128], src[:, 128 * c:128 * c + 128], ident)
                mm.then_inc(m_full, 1)

            def turn_h1(t):
                m_slot(t, ("p", "h1t"))
                pe.wait_ge(h1_done, t.p + 1)
                for c in range(4):
                    mm = pe.transpose(m_bank[:, 128 * c:128 * c + 128],
                                      h1[:, 2 * c:2 * c + 2, :].rearrange("p a o -> p (a o)"), ident)
                mm.then_inc(m_full, 1)

            def turn_logits(t):
                for i in range(NT):
                    mm = pe.transpose(m_bank[:, E * i:E * i + E], logits[:, 128 * i:128 * i + 128], ident[0:E, 0:E])
                mm.then_inc(m_full, 1)

            def turn_gates(t):
                m_slot(t, ("p", "gt"))
                pe.wait_ge(gw_done, t.p + 1)
                pe.transpose(m_bank[0:E * NT, 0:128], gw[:, :, :].rearrange("p e i -> p (e i)"), ident).then_inc(m_full, 1)

            def ffn_step(t, kind, ch):
                s = slice(ch * HALF, (ch + 1) * HALF)
                if (kind, ch) == ("s1", 0):
                    pe.wait_ge(h1t_done, 2 * t.p + 2)
                if kind == "s2":
                    pe.wait_ge(r_free, t.uses("r", ("p", "e3", ch)) + 4)
                bank = r_slot(t, ("p", kind, ch))
                if kind == "s1":
                    mm = pe.matmul(bank[0:64 + E, :], w("s1"), h1t[0:KW, s], start=True, stop=True)
                elif kind[0] == "e":
                    e = int(kind[1])
                    mm = pe.matmul(bank[:, :], w("e1")[:, 128 * e:128 * e + 128], h1t[0:KW, s], start=True, stop=True)
                elif kind == "s2":
                    mm = pe.matmul(bank[:, :], w("s2"), s1o[:, ch, :], start=True, stop=True)
                else:
                    for k in range(2):
                        e = 2 * int(kind[1]) + k
                        mm = pe.matmul(bank[64 * k:64 * k + 64, :], w("e2")[:, 64 * e:64 * e + 64], e1o[:, ch, e, :],
                                       start=True, stop=True)
                mm.then_inc(r_full, 1)

            def last_layer(t):
                bank = r_slot(t, ("p", "l3"))
                pe.wait_ge(gate_in, 80 * (t.p + 1))
                pe.wait_ge(r_free, t.uses("r", ("p", "s2", 1)) + 4)
                for k in range(4):
                    if k == 2:
                        pe.wait_ge(e2g_done, 4 * t.p + 4)
                    for ch in range(2):
                        lhs = (w("w3"), w("s3"), w("e3")[:, 0:64], w("e3")[:, 64:128])[k]
                        rhs = (h1t[:, ch * HALF:(ch + 1) * HALF], s2o[:, ch, :], e2g[:, ch, 0, :], e2g[:, ch, 1, :])[k]
                        mm = pe.matmul(bank[64 * ch:64 * ch + 64, :], lhs, rhs, start=(k == 0), stop=(k == 3))
                mm.then_inc(r_full, 1)

            def of_p(t, s):
                if s == T23_AT:
                    turn_heads(t, "p", 1)
                if s == TURN_OUTPUT_AT:
                    turn_output(t)
                if s == OUTPUT_AT:
                    output(t)
                if s == R1T_AT:
                    turn_residual(t, "r1t", r1)
                if s == H1T_AT:
                    turn_h1(t)
                if s == GATES_AT:
                    turn_gates(t)
                if s == R2T_AT:
                    turn_residual(t, "r2t", r2)

            def turn(t):
                for s in range(STAGES):
                    if t.a is not None:
                        scores(t, s)
                    if t.p is not None:
                        of_p(t, s)
                    maxima(t, BESIDE[s][:1])
                    if t.p is not None:
                        if s == LOGITS_AT:
                            m_slot(t, ("p", "gl"))
                            pe.wait_ge(logits_done, 2 * t.p + 2)
                        for kind, ch in FFN_AT.get(s, ()):
                            ffn_step(t, kind, ch)
                        if s == LOGITS_AT:
                            turn_logits(t)
                        if s == LAST_AT:
                            last_layer(t)
                    maxima(t, BESIDE[s][1:2])
                    if t.n is not None:
                        if s in TOKEN_STAGES and t is not FIRST_TURN:
                            tokens(t, TOKEN_STAGES.index(s), TOKEN_STAGES.index(s) + TOKEN_STAGES.count(s))
                        if s == V_AT:
                            project_v(t)
                    if s % NT == 1 and s > NT:
                        weigh(t, t.a, s // NT - 1, NT - 2) if t.a is not None else None
                        weigh(t, t.a, s // NT - 1, NT - 1) if t.a is not None else None
                    if s == 1 and t.p is not None:
                        weigh(t, t.p, H - 1, NT - 2)
                        weigh(t, t.p, H - 1, NT - 1)
                    if s % NT >= 2 and t.a is not None:
                        weigh(t, t.a, s // NT, s % NT - 2)
                    maxima(t, BESIDE[s][2:])
                    if s == QK_AT and t.n is not None:
                        project_qk(t)
                    if s == T01_AT and t.a is not None:
                        turn_heads(t, "a", 0)

            setup()
            tokens(PROLOGUE_TURN)
            pe.wait_ge(packed, 16)
            project_qk(PROLOGUE_TURN)
            project_v(PROLOGUE_TURN)
            tokens(FIRST_TURN, 0, 4)
            for k in range(4, 8):
                maxima(PROLOGUE_TURN, FIRST_MAX[2 * (k - 4):2 * (k - 4) + 2])
                tokens(FIRST_TURN, k, k + 1)
            maxima(PROLOGUE_TURN, FIRST_MAX[2 * (8 - 4):])
            run_turns(pe, turn)

        @block.scalar
        def _(act):
            def raw_tokens(t):
                act.wait_ge(token_full, 2 * t.n + 1)
                if t.a is not None:
                    act.wait_ge(res_done, t.a + 1)
                    act.wait_ge(hc_done, 2 * t.a + 2)
                for nn in range(2):
                    dst = raw[64:128, :].rearrange("p (i g v) -> p g i v", g=2, v=V)[:, nn]
                    act.activation(dst, token_bank[64 * nn:64 * nn + 64, :].rearrange("p (i v) -> p i v", v=V),
                                   ACT.Copy).then_inc(raw_done, 1)

            def first_parts(t):
                for c in range(2):
                    act.wait_ge(sm_full, t.uses("sm", ("n", "qk", c)) + 1)
                    bank = sm_bank[t.bank("sm", ("n", "qk", c), 2)]
                    act.activation(parts[:, 0, c * HALF:(c + 1) * HALF], bank[:, :], ACT.Copy).then_inc(p1_done, 1)

            def exponentials(t, s):
                for c in range(2):
                    if t.p is not None or s >= NPT:
                        act.wait_ge(pv_done, H * NT * t.a + s - NPT + 1)
                    key = ("a", "st", s, c)
                    act.wait_ge(r_full, t.uses("r", key) + 1)
                    act.activation(pt[:, s % NPT, c * HALF:(c + 1) * HALF], r_bank[t.bank("r", key, 3)][:, :], ACT.Exp,
                                   scale=SCALE).then_inc(r_free, 1)

            def turned_output(t):
                act.wait_ge(m_full, t.uses("m", ("p", "aot")) + 1)
                for k in range(2):
                    act.activation(comb[0:64, :].rearrange("p (i k n) -> p k i n", k=2, n=128)[:, k],
                                   m_bf[64 * k:64 * k + 64, 0:HALF].rearrange("p (i n) -> p i n", n=128),
                                   ACT.Copy).then_inc(comb_done, 1)

            def projected(t):
                act.wait_ge(m_full, t.uses("m", ("p", "wo")) + 1)
                act.activation(r1[:, :], m_bank[:, :], ACT.Identity, bias=w("bo")).then_inc(r1_done, 1)

            def squares(n):
                act.wait_ge(xc_done, n + 1)
                act.activation(sq[:, :, :], xc[:, :, :], ACT.Square).then_inc(sq_done, 1)

            def turned_h1(t):
                act.wait_ge(m_full, t.uses("m", ("p", "h1t")) + 1)
                for g in range(2):
                    act.activation(h1t[0:64, g * HALF:(g + 1) * HALF], m_bank[64 * g:64 * g + 64, :],
                                   ACT.Copy).then_inc(h1t_done, 1)

            def ffn_step(t, kind, ch):
                key = ("p", kind, ch)
                act.wait_ge(r_full, t.uses("r", key) + 1)
                bank = r_bank[t.bank("r", key, 3)]
                if kind == "s1":
                    dst, src, bias = s1o[0:64, ch, :], bank[0:64, :], 0.0
                    act.activation(logits[:, ch * HALF:(ch + 1) * HALF], bank[64:64 + E, :],
                                   ACT.Copy).then_inc(logits_done, 1)
                elif kind[0] == "e":
                    dst, src, bias = e1o[:, ch, int(kind[1]), :], bank[:, :], 0.0
                elif kind == "s2":
                    dst, src, bias = s2o[:, ch, :], bank[:, :], 0.0
                else:
                    k = int(kind[1])
                    dst, src, bias = e2o[:, ch, k, :], bank[:, :], w("eb2")[:, k:k + 1]
                act.activation(dst, src, ACT.Relu, bias=bias).then_inc(r_free, 1)

            def of_p(t, s):
                p = t.p
                for kind, ch in FFN_AT.get(s, ()):
                    ffn_step(t, kind, ch)
                if s == TURN_OUTPUT_AT:
                    turned_output(t)
                if s == OUTPUT_AT:
                    projected(t)
                if s == R1T_AT:
                    squares(2 * p)
                if s == H1T_AT:
                    turned_h1(t)
                if s == LOGITS_AT:
                    act.wait_ge(gd_done, 2 * p + 1)
                    act.activation(ge[:, :, :], gd[:, :, :], ACT.Exp).then_inc(ge_done, 1)
                if s == SHARE_AT:
                    act.wait_ge(gd_done, 2 * p + 2)
                    act.activation(gu[:, :, :], gd[:, :, :], ACT.Exp).then_inc(gu_done, 1)
                if s == GATES_AT:
                    act.wait_ge(m_full, t.uses("m", ("p", "gt")) + 1)
                    act.activation(gwt[:, :], m_bank[0:E * NT, 0:128], ACT.Copy).then_inc(gwt_done, 1)
                if s == LAST_AT:
                    key = ("p", "l3")
                    act.wait_ge(r_full, t.uses("r", key) + 1)
                    act.activation(r2[:, :], r_bank[t.bank("r", key, 3)][:, :], ACT.Copy).then_inc(r_free, 1)
                if s == R2T_AT:
                    squares(2 * p + 1)

            def turn(t):
                for s in range(STAGES):
                    if t.a is not None:
                        exponentials(t, s)
                    if t.p is not None:
                        of_p(t, s)
                    if t.n is not None:
                        if s == TOKEN_STAGES[-1] and t is not FIRST_TURN:
                            raw_tokens(t)
                        if s == QK_AT:
                            first_parts(t)

            act.wait_ge(token_packed, 16)
            act.activation(ident_bf[:, :], ident, ACT.Copy).then_inc(ident_set, 1)
            act.wait_ge(mt_full, 1)
            for half in range(2):
                dst, src = token_weight_halves(1, half)
                act.activation(dst, src, ACT.Copy).then_inc(mt_read, 1)
            act.wait_ge(packed, 16)
            raw_tokens(PROLOGUE_TURN)
            first_parts(PROLOGUE_TURN)
            raw_tokens(FIRST_TURN)
            run_turns(act, turn)

        @block.vector
        def _(dve):
            taken = [0, 0, 0]

            def step(ins):
                taken[1] += 1
                ins.then_inc(dve_step, 1)
                dve.wait_ge(dve_step, DVE_STEPS * taken[2] + (taken[0] + taken[1]))

            def setup():
                dve.memset(later[:, :, 0:1], 3.0).then_inc(sm_free, 2)
                dve.memset(later[:, :, 1:2], 2.0).then_inc(r_free, 3)
                dve.memset(later[:, :, 2:3], 1.0).then_inc(y_out, 1)
                step(dve.memset(later[:, :, 3:4], 0.0))
                dve.wait_ge(mt_full, 1)
                for half in range(2):
                    dst, src = token_weight_halves(0, half)
                    dve.tensor_copy(dst, src).then_inc(mt_read, 1)
                dve.wait_ge(wt_full, 1)
                dve.tensor_copy(wtok[:, :, :].rearrange("p k o -> p (k o)"), m_bank[:, :]).then_inc(wt_read, 1)
                dve.wait_ge(pool_set, 9)

            def clip(t):
                dve.wait_ge(raw_done, 2 * t.n + 2)
                for c in range(2):
                    s = slice(c * HALF, (c + 1) * HALF)
                    dve.tensor_scalar(hc[0:64, s], raw[64:128, s], CLIP, -CLIP, ALU.min, ALU.max).then_inc(hc_done, 1)

            def rest_of(t, c):
                s = slice(c * HALF, (c + 1) * HALF)
                key = ("n", "qk", c)
                dve.wait_ge(p1_done, 2 * t.n + c + 1)
                dve.tensor_tensor(rest[:, s], sm_bank[t.bank("sm", key, 2)][:, :], parts[:, 0, s],
                                  ALU.subtract).then_inc(sm_free, 1)
                dve.wait_ge(sm_free, t.uses("sm", key) + 3)
                dve.tensor_copy(parts[:, 1, s], rest[:, s]).then_inc(p2_done, 1)

            def values(t):
                dve.wait_ge(token_full, 2 * t.n + 2)
                dve.tensor_copy(vst[:, :, :].rearrange("p i d -> p (i d)"), token_bank[:, :]).then_inc(val_done, 1)

            def max_tile(t, key):
                h, m, c = key[2:]
                dve.wait_ge(sm_full, t.uses("sm", key) + 1)
                dve.tensor_reduce(mx2[:, h, m, c:c + 1], sm_bank[t.bank("sm", key, 2)][:, :], AX.X, ALU.max).then_inc(sm_free, 1)
                if (m, c) == (NT - 1, 1):
                    dve.wait_ge(sm_free, t.uses("sm", key) + 3)
                    dve.tensor_reduce(ngm[:, h, :], mx2[:, h, :, :], AX.X, ALU.max, negate=True).then_inc(max_done, 1)

            def split_max(t, key):
                h = key[2]
                bank = sm_bank[t.bank("sm", key, 2)][0:NT, 0:128]
                dve.wait_ge(sm_full, t.uses("sm", key) + 1)
                step(dve.tensor_copy(mpart[:, h % 2, 0, :], bank))
                dve.tensor_tensor(mrest[:, :], bank, mpart[:, h % 2, 0, :], ALU.subtract).then_inc(sm_free, 1)
                dve.wait_ge(sm_free, t.uses("sm", key) + 3)
                step(dve.tensor_copy(mpart[:, h % 2, 1, :], mrest[:, :]))
                dve.tensor_tensor(mpart[:, h % 2, 2, :], mrest[:, :], mpart[:, h % 2, 1, :],
                                  ALU.subtract).then_inc(mpart_done, 1)

            def maxima(t, keys):
                for key in keys:
                    if key in t.seq["sm"]:
                        (split_max if key[1] == "t" else max_tile)(t, key)

            def head_out(b, h):
                dve.wait_ge(pv_done, H * NT * b + NT * (h + 1))
                dve.tensor_copy(osb[:, h, :], ot_bank[:, 0:256]).then_inc(osb_done, 1)

            def divide(t, who, p):
                b = t.p if who == "p" else t.a
                dve.wait_ge(m_full, t.uses("m", (who, ("t01", "t23")[p])) + 1)
                turned = m_bank[:, :].rearrange("p (k a j d) -> p k a j d", k=2, a=2, j=4)
                step(dve.reciprocal(rec[:, p, :, :].rearrange("p k n -> p (k n)"),
                                       m_bank[:, :].rearrange("p (n d) -> p n d", d=32)[:, :, DH]))
                for k in range(2):
                    h = 2 * p + k
                    dst = ao[:, :, DH * h:DH * h + DH].rearrange("p (j a) d -> p a j d", a=2)
                    dve.tensor_tensor(dst, turned[:, k, :, :, 0:DH],
                                      rec[:, p, k, :].rearrange("p (a j) -> p a j", a=2).unsqueeze(3)
                                      .to_broadcast([128, 2, 4, DH]), ALU.mult).then_inc(ao_done, 1)

            def spread(v):
                return v.unsqueeze(2).to_broadcast([128, NT, D])

            def centre(t, name):
                dve.wait_ge(m_full, t.uses("m", ("p", name)) + 1)
                r = m_bank[:, :].rearrange("p (g o) -> p g o", o=D)
                step(dve.tensor_reduce(st[:, 0, :], r, AX.X, ALU.add))
                dve.scalar_tensor_tensor(out=xc[:, :, :], in0=spread(st[:, 0, :]), scalar=-1.0 / D, in1=r,
                                         op0=ALU.mult, op1=ALU.add).then_inc(xc_done, 1)

            def variance(n):
                dve.wait_ge(sq_done, n + 1)
                step(dve.tensor_reduce(st[:, 2, :], sq[:, :, :], AX.X, ALU.add))
                dve.tensor_scalar(st[:, 3, :], st[:, 2, :], 1.0 / D, EPS, ALU.mult, ALU.add).then_inc(var_done, 1)

            def first_norm(b):
                dve.wait_ge(rstd_done, 2 * b + 2)
                dve.tensor_tensor(h1[:, :, :], xc[:, :, :], spread(st[:, 4, :]), ALU.mult).then_inc(h1_done, 1)

            def second_norm(b):
                dve.wait_ge(rstd_done, 2 * b + 3)
                dve.wait_ge(y_out, 32 * b + 1)
                dve.tensor_tensor(y[:, :, :].rearrange("p (a c) o -> p c a o", a=2),
                                  xc[:, :, :].rearrange("p (c a) o -> p c a o", a=2),
                                  st[:, 4, :].rearrange("p (c a) -> p c a", a=2).unsqueeze(3)
                                  .to_broadcast([128, 4, 2, D]), ALU.mult).then_inc(y_done, 1)

            def over(v):
                return v.unsqueeze(2).to_broadcast([128, NT, E])

            def less_maximum(t):
                b = t.p
                dve.wait_ge(m_full, t.uses("m", ("p", "gl")) + 1)
                dve.tensor_copy(gl[:, :, :].rearrange("p i e -> p (i e)"), m_bank[:, 0:NT * E]).then_inc(gl_done, 1)
                dve.wait_ge(gl_done, b + 1)
                step(dve.tensor_reduce(gs[:, 0, :], gl[:, :, :], AX.X, ALU.max))
                dve.tensor_tensor(gd[:, :, :], gl[:, :, :], over(gs[:, 0, :]), ALU.subtract).then_inc(gd_done, 1)

            def shares(b):
                dve.wait_ge(ge_done, b + 1)
                step(dve.tensor_reduce(gs[:, 1, :], ge[:, :, :], AX.X, ALU.add))
                step(dve.reciprocal(gs[:, 2, :], gs[:, 1, :]))
                step(dve.tensor_tensor(gp[:, :, :], ge[:, :, :], over(gs[:, 2, :]), ALU.mult))
                step(dve.tensor_reduce(gs[:, 3, :], gp[:, :, :], AX.X, ALU.max))
                dve.tensor_tensor(gd[:, :, :], gp[:, :, :], over(gs[:, 3, :]), ALU.subtract).then_inc(gd_done, 1)

            def rank_gates():
                for k in range(1, E):
                    step(dve.tensor_tensor(gc[:, k, :, 0:E - k], gp[:, :, 0:E - k], gp[:, :, k:E], ALU.is_ge))
                for k in range(1, E):
                    if k == 1:
                        step(dve.tensor_tensor(rank[:, :, 0:E - 1], later[:, :, 0:E - 1], gc[:, 1, :, 0:E - 1],
                                                  ALU.subtract))
                        step(dve.tensor_copy(rank[:, :, E - 1:E], later[:, :, E - 1:E]))
                    else:
                        step(dve.tensor_tensor(rank[:, :, 0:E - k], rank[:, :, 0:E - k], gc[:, k, :, 0:E - k],
                                                  ALU.subtract))
                    step(dve.tensor_tensor(rank[:, :, k:E], rank[:, :, k:E], gc[:, k, :, 0:E - k], ALU.add))

            def choose(b):
                dve.wait_ge(gu_done, b + 1)
                step(dve.scalar_tensor_tensor(out=gm[:, :, :], in0=rank[:, :, :], scalar=2.0, in1=gu[:, :, :],
                                                 op0=ALU.is_lt, op1=ALU.mult))
                step(dve.tensor_reduce(gs[:, 4, :], gm[:, :, :], AX.X, ALU.add))
                step(dve.reciprocal(gs[:, 5, :], gs[:, 4, :]))
                dve.tensor_tensor(gw[:, :, :].rearrange("p e i -> p i e"), gm[:, :, :], over(gs[:, 5, :]),
                                  ALU.mult).then_inc(gw_done, 1)

            def weigh_experts(t, ch):
                b = t.p
                if ch == 0:
                    dve.wait_ge(gate_in, 80 * (b + 1))
                for k in range(2):
                    dve.wait_ge(r_free, t.uses("r", ("p", f"p{k}", ch)) + 4)
                    dve.tensor_tensor(e2g[:, ch, k, :], e2o[:, ch, k, :], wgb[:, k, ch * HALF:(ch + 1) * HALF],
                                      ALU.mult).then_inc(e2g_done, 1)

            def of_p(t, s):
                p = t.p
                if s == 2:
                    head_out(p, H - 1)
                if s == T23_AT:
                    divide(t, "p", 1)
                if s == R1T_AT:
                    centre(t, "r1t")
                if s == VAR1_AT:
                    variance(2 * p)
                if s == NORM1_AT:
                    first_norm(p)
                if s == LOGITS_AT:
                    less_maximum(t)
                if s == SHARE_AT:
                    shares(p)
                if s == RANK_AT:
                    rank_gates()
                if s == CHOOSE_AT:
                    choose(p)
                if s in WEIGH_AT:
                    weigh_experts(t, WEIGH_AT[s])
                if s == R2T_AT:
                    centre(t, "r2t")
                if s == VAR2_AT:
                    variance(2 * p + 1)
                if s == NORM2_AT:
                    second_norm(p)

            def turn(t):
                taken[:] = taken[0] + taken[1], 0, (t.p if t.kind == "loop" else 0)
                if t.kind == "last":
                    taken[0] += DVE_STEPS * (B - 3)
                for s in range(STAGES):
                    if t.p is not None:
                        of_p(t, s)
                    if t.n is not None and s == CLIP_AT:
                        clip(t)
                    if s % NT == 2 and s > NT and t.a is not None:
                        head_out(t.a, s // NT - 1)
                    maxima(t, BESIDE[s])
                    if t.n is not None:
                        if s == QK_AT:
                            rest_of(t, 0)
                            rest_of(t, 1)
                        if s == V_AT:
                            values(t)
                    if s == T01_AT and t.a is not None:
                        divide(t, "a", 0)
                assert t.kind != "loop" or taken[1] == DVE_STEPS, taken[1]

            setup()
            clip(PROLOGUE_TURN)
            rest_of(PROLOGUE_TURN, 0)
            rest_of(PROLOGUE_TURN, 1)
            values(PROLOGUE_TURN)
            maxima(PROLOGUE_TURN, FIRST_MAX)
            run_turns(dve, turn)


def packed_weights(a):
    import numpy as np

    pack = np.zeros((128, PACK_COLS), np.float32)

    def put(name, value, r0=0, c0=0):
        value = np.asarray(value)
        at = PACK[name][1]
        pack[r0:r0 + value.shape[0], at + c0:at + c0 + value.shape[1]] = value

    by_dim = np.arange(D).reshape(H, DH).T.reshape(-1)
    put("ident", np.eye(128))
    for n, k in enumerate("qk"):
        put("wqk", a[f"L0_attn_W{k}"][by_dim].T, 0, D * n)
        put("wqk", a[f"L0_attn_b{k}"][by_dim][None], D, D * n)
    put("wv", a["L0_attn_Wv"].T)
    put("wv", a["L0_attn_bv"][None], D)
    put("wo", a["L0_attn_Wo"].T)
    put("wo", np.eye(D), D)
    put("bo", a["L0_attn_bo"][:, None])
    put("bo", a["L0_attn_bo"][:, None], D)
    put("s1", a["L0_ffn_sW1"])
    put("s1", a["L0_ffn_sb1"][None], D)
    put("s1", a["L0_ffn_gW"], 0, D)
    put("s1", a["L0_ffn_gb"][None], D, D)
    put("s2", a["L0_ffn_sW2"])
    put("s2", a["L0_ffn_sb2"][None], D)
    put("s3", a["L0_ffn_sW3"])
    put("w3", np.eye(D))
    put("w3", a["L0_ffn_sb3"][None], D)
    put("w3", a["L0_ffn_eb3"], KW)
    for e in range(E):
        put("e1", a["L0_ffn_eW1"][e], 0, 128 * e)
        put("e1", a["L0_ffn_eb1"][e][None], D, 128 * e)
        put("e2", a["L0_ffn_eW2"][e], 0, 64 * e)
        put("eb2", a["L0_ffn_eb2"][e][:, None], 64 * (e % 2), e // 2)
        put("e3", a["L0_ffn_eW3"][e], 64 * (e % 2), 64 * (e // 2))
    angle = 2 * np.pi * np.arange(RF // 2)[:, None] * np.arange(PATCH)[None] / PATCH
    dft = np.concatenate([np.cos(angle), -np.sin(angle)]) / np.sqrt(PATCH)
    dft[np.abs(dft) < 1e-12] = 0.0
    tok = a["L0_tok_W"].reshape(D, RF, C // CG, CG)
    for c in range(CG):
        put("dft", dft, RF * c, PATCH * c)
        put("wt", tok[:, :, :, c].transpose(1, 2, 0).reshape(RF, -1), RF * c)
    return pack


def kernel(**inputs):
    import numpy as np
    import concourse.bacc as bacc
    from concourse.bass_utils import run_bass_kernel_spmd

    a = {k: np.asarray(v) for k, v in inputs.items()}
    arrays = {"x": np.ascontiguousarray(a["x"]), "pack": packed_weights(a)}
    nc = bacc.Bacc("TRN2", target_bir_lowering=False, num_devices=1)
    args = [nc.dram_tensor(n, v.shape, mybir.dt.from_np(v.dtype), kind="ExternalInput").ap() for n, v in arrays.items()]
    out = nc.dram_tensor("out", (B, N, D), F32, kind="ExternalOutput").ap()
    vit_layer(nc, *args, out)
    r = run_bass_kernel_spmd(nc, [arrays], core_ids=[0])
    return r.results[0]["out"]
```

```python
from contextlib import ExitStack

import concourse.bass as bass
from concourse import mybir

F32 = mybir.dt.float32
BF16 = mybir.dt.bfloat16
ALU = mybir.AluOpType
ACT = mybir.ActivationFunctionType
AX = mybir.AxisListType

B, C, T, V = 4, 64, 128, 64
PATCH, STRIDE, NPATCH = 16, 8, 16
RF = PATCH + 2
CG = 4
N = V * NPATCH
D, H, DH = 64, 4, 16
NT = N // 128
HALF = N // 2
E = 4
SCALE = float(DH) ** -0.5
CLIP = 10000.0
EPS = 1e-5
TERMS_Q = (0, 1, 2, 0, 1, 0)
TERMS_K = (2, 1, 0, 1, 0, 0)
RUNS = ((0, 3), (3, 5), (5, 6))
KS = 16 * len(TERMS_Q)
KM = KS + 3
GATE_ROW = 96

PACK, _at = {}, 0
for _name, _rows, _cols in (
    ("ident", 128, 128), ("dft", 128, CG * PATCH), ("wt", 128, 16 * 64), ("wqk", 128, 128), ("wv", 128, 64),
    ("wo", 128, 64), ("bo", 128, 1),
    ("s1", 128, 64 + E), ("e1", 128, 128 * E), ("s2", 128, 128), ("e2", 128, 64 * E), ("eb2", 128, 2),
    ("w3", 128, 64), ("s3", 128, 64), ("e3", 128, 128),
):
    PACK[_name] = (_rows, _at, _cols)
    _at += _cols
PACK_COLS = _at
TOKEN_COLS = PACK["wqk"][1]

STAGES = H * NT
T23_AT, TURN_OUTPUT_AT, OUTPUT_AT, R1T_AT, VAR1_AT, NORM1_AT, H1T_AT = 3, 4, 5, 6, 7, 8, 9
TOKEN_STAGES = (7, 7, 7, 7, 8, 8, 8, 8)
CLIP_AT, QK_AT, LOGITS_AT, V_AT = 8, 10, 11, 12
VT_AT = V_AT + 1
EARLY_TOKENS = 5
SHARE_AT, RANK_AT, CHOOSE_AT, GATES_AT = 12, 13, 14, 15
WEIGH_AT = {19: 0, 24: 1}
LAST_AT, R2T_AT, T01_AT, VAR2_AT, NORM2_AT = 25, 27, 28, 28, 30
FFN_STEPS = [("s1", 0), ("s1", 1)] + [(k, ch) for ch in range(2) for k in ("e0", "e1", "e2", "e3", "s2", "p0", "p1")]
STEP_STAGES = (10, 10, 11, 14, 14, 14, 16, 18, 18, 19, 19, 20, 21, 22, 23, 24)
FFN_AT = {_s: [k for k, at in zip(FFN_STEPS, STEP_STAGES) if at == _s] for _s in range(STAGES)}
assert FFN_AT[LOGITS_AT]
FFN_ALONE_AT = {STEP_STAGES[0] + _n: [k] for _n, k in enumerate(FFN_STEPS)}
ALONE_LOGITS_AT, ALONE_SHARE_AT, ALONE_GATES_AT = (STEP_STAGES[0] + _n for _n in (2, 4, 8))

AHEAD1 = 8

def _head_tiles(who, h):
    return [(who, "sm", h, m, c) for m in range(NT) for c in range(2)]


_n0, _n1 = _head_tiles("n", 0), _head_tiles("n", 1)[:AHEAD1]
NEXT_MAX = _n0[2:] + _n1[:2] + [("n", "t", 0)] + _n1[2:]
_line = _head_tiles("a", 1)[AHEAD1:]
for _h in (2, 3):
    _line += _head_tiles("a", _h)[:2] + [("a", "t", _h - 1)] + _head_tiles("a", _h)[2:]
_line += _n0[:2] + [("a", "t", 3)] + NEXT_MAX
FIRST_MAX = _n0[:2] + NEXT_MAX
COUNTS = (2, 3, 3, 2, 3, 4, 1, 2, 2, 1, 3, 1, 1, 1, 2, 3, 2, 3, 2, 3, 1, 2, 3, 3, 2, 2, 3, 3, 1, 1, 2, 1)
BESIDE = {}
for _s in range(STAGES):
    BESIDE[_s], _line = _line[:COUNTS[_s]], _line[COUNTS[_s]:]
assert not _line

SM_SEQ, R_SEQ = [], []
for _s in range(STAGES):
    SM_SEQ += [("n", "vt")] if _s == V_AT else []
    SM_SEQ += [("n", "v")] if _s == VT_AT else []
    SM_SEQ += BESIDE[_s] + ([("n", "qk", 0), ("n", "qk", 1)] if _s == QK_AT else [])
    R_SEQ += [("a", "st", _s, c) for c in range(2)] + [("p", *k) for k in FFN_AT.get(_s, ())]
    R_SEQ += [("p", "l3")] if _s == LAST_AT else []
_of_stage = (("p", "t23", T23_AT), ("p", "aot", TURN_OUTPUT_AT), ("p", "wo", OUTPUT_AT), ("p", "r1t", R1T_AT),
             ("p", "h1t", H1T_AT), ("p", "gt", GATES_AT), ("p", "r2t", R2T_AT), ("p", "gl", LOGITS_AT),
             ("n", "tok", TOKEN_STAGES[0]), ("a", "t01", T01_AT))
M_SEQ = [e[:2] for e in sorted(_of_stage, key=lambda e: e[2])]
PROLOGUE = {"sm": [("n", "qk", 0), ("n", "qk", 1), ("n", "vt"), ("n", "v")] + FIRST_MAX, "r": [],
            "m": [("n", "tok")]}
SEQ = {"sm": SM_SEQ, "r": R_SEQ, "m": M_SEQ}
assert len(SM_SEQ) % 3 == 0 and len(R_SEQ) % 3 == 0


class Turn:

    def __init__(self, p, a, n, kind):
        self.p, self.a, self.n, self.kind = p, a, n, kind
        have = [k for k, v in (("p", p), ("a", a), ("n", n)) if v is not None]
        self.seq = PROLOGUE if kind == "prologue" else {r: [e for e in q if e[0] in have] for r, q in SEQ.items()}
        alone = kind == "epilogue"
        self.ffn_at = FFN_ALONE_AT if alone else FFN_AT
        end = max(FFN_ALONE_AT)
        self.logits_at, self.share_at, self.gates_at, self.last_at, self.r2t_at = (
            (ALONE_LOGITS_AT, ALONE_SHARE_AT, ALONE_GATES_AT, end + 1, end + 2) if alone else
            (LOGITS_AT, SHARE_AT, GATES_AT, LAST_AT, R2T_AT))
        self.start = {}
        for r, q in SEQ.items():
            first = len(PROLOGUE[r])
            second = first + len([e for e in q if e[0] != "p"])
            last = second + (B - 2) * len(q)
            after = last + len([e for e in q if e[0] != "n"])
            self.start[r] = {"prologue": 0, "first": first, "loop": second, "last": last, "epilogue": after}[kind]

    def bank(self, ring, key, banks):
        return (self.start[ring] + self.seq[ring].index(key)) % banks

    def uses(self, ring, key=None):
        n = self.start[ring] + (self.seq[ring].index(key) if key else 0)
        return n + len(SEQ[ring]) * self.p if self.kind == "loop" else n


def run_turns(engine, turn):
    turn(FIRST_TURN)
    with engine.Fori(0, B - 2) as b:
        turn(Turn(b, b + 1, b + 2, "loop"))
    turn(Turn(B - 2, B - 1, None, "last"))
    turn(Turn(B - 1, None, None, "epilogue"))


PROLOGUE_TURN = Turn(None, None, 0, "prologue")
FIRST_TURN = Turn(None, 0, 1, "first")
DVE_STEPS = 32
NPT = 4


def vit_layer(nc, x, pack, out):
    with ExitStack() as ctx:
        def sb(name, shape, dt=F32):
            return ctx.enter_context(nc.sbuf_tensor(name, shape, dt))

        def sem(name):
            return ctx.enter_context(nc.semaphore(name))

        banks = [ctx.enter_context(nc.psum_tensor(f"bank{i}", [128, 512], F32)) for i in range(8)]
        sm_bank, r_bank, ot_bank, m_bank = banks[0:3], banks[3:6], banks[6], banks[7]
        m_bf = m_bank[:, :].bitcast(BF16)

        qk_dram = nc.dram_tensor("qk_dram", (2, 3 * DH, H * N), BF16)
        mx_dram = nc.dram_tensor("mx_dram", (H, NT, 3, 128), BF16)
        gate_dram = nc.dram_tensor("gate_dram", (E, N), F32)

        pk = sb("pk", [128, PACK_COLS])

        def w(name, r0=0, r1=None):
            rows, at, cols = PACK[name]
            return pk[r0:rows if r1 is None else r1, at:at + cols]

        ident = w("ident")
        ident_bf = sb("ident_bf", [128, 128], BF16)
        mt = sb("mt", [64, CG * 16 * PATCH])
        wtok = sb("wtok", [128, 8, 64])
        xs = sb("xs", [128, NPATCH + 1, 4 * V])
        raw = sb("raw", [128, N])
        vt = sb("vt", [128, HALF])
        vst = sb("vst", [128, NT, D])
        comb = sb("comb", [128, N])
        hc = sb("hc", [128, N])
        vv = sb("vv", [128, NT, H, 32])
        parts = sb("parts", [128, 3, N], BF16)
        rest = sb("rest", [128, N])
        qst = sb("qst", [KM, H, N], BF16)
        kst = sb("kst", [KM, H, N], BF16)
        pt = sb("pt", [128, NPT, N])
        mx2 = sb("mx2", [128, H, NT, 2])
        ngm = sb("ngm", [128, H, NT])
        mrest = sb("mrest", [NT, 128])
        mpart = sb("mpart", [NT, 2, 3, 128], BF16)
        osb = sb("osb", [128, H, 256])
        rec = sb("rec", [128, 2, 2, 8])
        ao = sb("ao", [128, NT, D], BF16)
        r1 = sb("r1", [128, HALF])
        r2 = sb("r2", [128, HALF])
        xc = sb("xc", [128, NT, D])
        sq = sb("sq", [128, NT, D])
        st = sb("st", [128, 5, NT])
        halfpow = sb("halfpow", [128, NT])
        zero = sb("zero", [128, NT * H])
        h1 = sb("h1", [128, NT, D])
        h1t = sb("h1t", [128, N])
        y = sb("y", [128, NT, D])
        s1o = sb("s1o", [128, 2, HALF])
        logits = sb("logits", [E, N])
        s2o = sb("s2o", [128, 2, HALF])
        e1o = sb("e1o", [128, 2, E, HALF])
        e2o = sb("e2o", [128, 2, 2, HALF])
        e2g = sb("e2g", [128, 2, 2, HALF])
        wgb = sb("wgb", [128, 2, N])
        gl = sb("gl", [128, NT, E])
        gd = sb("gd", [128, NT, E])
        ge = sb("ge", [128, NT, E])
        gp = sb("gp", [128, NT, E])
        gu = sb("gu", [128, NT, E])
        later = sb("later", [128, NT, E])
        rank = sb("rank", [128, NT, E])
        gm = sb("gm", [128, NT, E])
        gc = sb("gc", [128, E, NT, E])
        gs = sb("gs", [128, 6, NT])
        gw = sb("gw", [128, E, NT])
        gwt = sb("gwt", [E * NT, 128])

        token_packed = sem("token_packed")
        packed, x_in, stack01_in, stack23_in, mrow_out, mrow_in = (
            sem(n) for n in ("packed", "x_in", "stack01_in", "stack23_in", "mrow_out", "mrow_in"))
        parts_out, gate_out, gate_in, y_out = (sem(n) for n in ("parts_out", "gate_out", "gate_in", "y_out"))
        gate_rows_in = sem("gate_rows_in")
        ident_set, mt_full, mt_read, wt_full, wt_read, pool_set = (
            sem(n) for n in ("ident_set", "mt_full", "mt_read", "wt_full", "wt_read", "pool_set"))
        sm_full, sm_free, r_full, r_free, m_full = (sem(n) for n in ("sm_full", "sm_free", "r_full", "r_free", "m_full"))
        res_done, p1_done, p2_done, p3_done = (sem(n) for n in ("res_done", "p1_done", "p2_done", "p3_done"))
        raw_done, hc_done, pv_done, osb_done, ao_done = (
            sem(n) for n in ("raw_done", "hc_done", "pv_done", "osb_done", "ao_done"))
        max_done, mpart_done, comb_done, r1_done = (sem(n) for n in ("max_done", "mpart_done", "comb_done", "r1_done"))
        xc_done, sq_done, var_done, rstd_done, h1_done, h1t_done, y_done = (
            sem(n) for n in ("xc_done", "sq_done", "var_done", "rstd_done", "h1_done", "h1t_done", "y_done"))
        logits_done, vv_done = (sem(n) for n in ("logits_done", "vv_done"))
        gl_done, gd_done, ge_done, gu_done, gw_done, gwt_done, e2g_done = (
            sem(n) for n in ("gl_done", "gd_done", "ge_done", "gu_done", "gw_done", "gwt_done", "e2g_done"))
        dve_step = sem("dve_step")

        block = ctx.enter_context(nc.Block())

        x_v = x.rearrange("b c (n g j) v -> b g c n (j v)", n=NPATCH, g=2, j=4)
        x_last = x[:, :, T - 1, :]
        out_v = out.rearrange("b (v g i) o -> b g v (i o)", v=V, g=2, i=NT)

        def token_weight_halves(k, half):
            src = (ot_bank, r_bank[0])[k][0:64, :].rearrange("o (c k g j) -> o k j g c", k=2, g=2, j=4)
            dst = mt[:, :].rearrange("o (k j g c) -> o k j g c", k=2, j=4, g=2)
            return dst[:, half, :, :, 32 * k:32 * k + 32], src[:, half]

        @block.sync
        def _(sp):
            def load_x(b):
                for g in range(2):
                    sp.dma_start(xs[64 * g:64 * g + 64, 0:NPATCH, :], x_v[b, g]).then_inc(x_in, 16)
                    sp.dma_start(xs[64 * g:64 * g + 64, NPATCH, :].rearrange("p (j v) -> p j v", j=4),
                                 x_last[b].unsqueeze(1).to_broadcast([64, 4, V])).then_inc(x_in, 16)

            def parts_to_dram(b, first=False):
                if not first:
                    sp.wait_ge(stack23_in, 96 * b)
                for part, done in enumerate((p1_done, p2_done, p3_done)):
                    sp.wait_ge(done, 2 * b + 2)
                    for side in range(2):
                        place = (2 - part if side else part) * DH
                        sp.dma_start(qk_dram[side, place:place + DH, :].rearrange("d (h n) -> (d h) n", h=H),
                                     parts[64 * side:64 * side + 64, part, :]).then_inc(parts_out, 16)

            def stacks(b, h0):
                sp.wait_ge(parts_out, 96 * (b + 1))
                for side, dst in enumerate((qst, kst)):
                    for t0, t1 in RUNS:
                        r0 = DH * (2 - TERMS_K[t0] if side else TERMS_Q[t0])
                        arrived = stack23_in if h0 else stack01_in
                        sp.dma_start(dst[DH * t0:DH * t1, h0:h0 + 2, :].rearrange("p h n -> p (h n)"),
                                     qk_dram[side, r0:r0 + DH * (t1 - t0), N * h0:N * h0 + 2 * N]).then_inc(arrived, 16)

            def max_rows(b, h):
                sp.wait_ge(mpart_done, H * b + h + 1)
                sp.dma_start(mx_dram[h], mpart[:, h % 2, :, :]).then_inc(mrow_out, 16)
                sp.wait_ge(mrow_out, 16 * (H * b + h + 1))
                sp.dma_start(qst[KS:KM, h, :].rearrange("p (j n) -> p j n", j=NT),
                             mx_dram[h].rearrange("j t n -> t j n")).then_inc(mrow_in, 16)

            def gates(b):
                sp.wait_ge(gwt_done, b + 1)
                sp.dma_start(gate_dram.ap().rearrange("e (i n) -> (e i) n", i=NT), gwt[:, :]).then_inc(gate_out, 16)
                sp.wait_ge(gate_out, 16 * (b + 1))
                for e in range(E):
                    sp.dma_start(wgb[64 * (e % 2):64 * (e % 2) + 64, e // 2, :],
                                 gate_dram[e:e + 1, :].to_broadcast([64, N])).then_inc(gate_in, 16)

            def gate_rows(t):
                sp.wait_ge(r_full, t.uses("r", ("p", "e3", 1)) + 1)
                sp.dma_start(h1t[GATE_ROW:GATE_ROW + E, :], gate_dram.ap()).then_inc(gate_rows_in, 16)

            def store(b):
                sp.wait_ge(y_done, b + 1)
                for g in range(2):
                    sp.dma_start(out_v[b, g], y[64 * g:64 * g + 64, :, :].rearrange("p i o -> p (i o)")).then_inc(y_out, 16)

            def turn(t):
                p, a, n = t.p, t.a, t.n
                if p is not None and a is not None:
                    sp.wait_ge(r_full, t.uses("r"))
                    stacks(a, 2)
                if n is not None and t is not FIRST_TURN:
                    sp.wait_ge(raw_done, 2 * a + 2)
                    load_x(n)
                if a is not None:
                    max_rows(a, 1)
                if n is not None:
                    parts_to_dram(n)
                if a is not None:
                    max_rows(a, 2)
                if p is not None:
                    gates(p)
                if n is not None:
                    sp.wait_ge(r_full, t.uses("r", ("a", "st", 2 * NT - 1, 1)) + 1)
                    stacks(n, 0)
                if a is not None:
                    max_rows(a, 3)
                if p is not None:
                    gate_rows(t)
                if n is not None:
                    max_rows(n, 0)
                if p is not None:
                    store(p)

            sp.dma_start(pk[:, 0:TOKEN_COLS], pack[:, 0:TOKEN_COLS]).then_inc(token_packed, 16)
            load_x(0)
            sp.dma_start(pk[:, TOKEN_COLS:], pack[:, TOKEN_COLS:]).then_inc(packed, 16)
            sp.wait_ge(raw_done, 2)
            load_x(1)
            parts_to_dram(0, first=True)
            stacks(0, 0)
            stacks(0, 2)
            max_rows(0, 0)
            run_turns(sp, turn)
            sp.wait_ge(y_out, 32 * B + 1)

        @block.gpsimd
        def _(pool):
            for n, (dst, value) in enumerate((
                    (hc[64:128, :], 0.0), (h1t[64:128, :], 0.0), (s1o[64:128, :, :], 0.0),
                    (hc[64:65, :], 1.0), (h1t[64:65, :], 1.0), (s1o[64:65, :, :], 1.0), (vv[:, :, :, 16:32], 1.0),
                    (kst[KS:KM, :, :], 1.0), (halfpow[:, :], -0.5))):
                if n:
                    pool.wait_ge(pool_set, n)
                pool.memset(dst, value).then_inc(pool_set, 1)
            pool.wait_ge(pool_set, 9)
            pool.memset(zero[:, :], 0.0).then_inc(rstd_done, 1)
            pool.wait_ge(rstd_done, 1)

            def third_parts(b, first=False):
                if not first:
                    pool.wait_ge(res_done, b)
                for c in range(2):
                    s = slice(c * HALF, (c + 1) * HALF)
                    pool.wait_ge(p2_done, 2 * b + c + 1)
                    pool.tensor_tensor(parts[:, 2, s], rest[:, s], parts[:, 1, s], ALU.subtract).then_inc(p3_done, 1)

            def rstd(n):
                pool.wait_ge(var_done, n + 1)
                pool.tensor_tensor(st[:, 4, :], st[:, 3, :], halfpow[:, :], ALU.pow).then_inc(rstd_done, 1)

            def turn(t):
                p, a, n = t.p, t.a, t.n
                if a is not None:
                    if p is not None:
                        pool.wait_ge(rstd_done, 2 * p + 1)
                        pool.wait_ge(pv_done, H * NT * a)
                    pool.wait_ge(max_done, H * a + 1)
                    kept = vst[:, :, :].rearrange("p i (h d) -> p (i h) d", d=DH)
                    pool.tensor_tensor(vv[:, :, :, 0:DH].rearrange("p i h d -> p (i h) d"), kept,
                                       zero[:, :].unsqueeze(2).to_broadcast([128, NT * H, DH]),
                                       ALU.subtract).then_inc(vv_done, 1)
                    if p is not None:
                        pool.wait_ge(m_full, t.uses("m", ("p", "wo")) + 1)
                    pool.wait_ge(raw_done, 2 * a + 2)
                    pool.wait_ge(vv_done, a + 1)
                    pool.tensor_tensor(comb[64:128, :], raw[64:128, :], zero[64:128, 0:1].to_broadcast([64, N]),
                                       ALU.subtract).then_inc(res_done, 1)
                if p is not None:
                    if a is not None:
                        pool.wait_ge(res_done, a + 1)
                    rstd(2 * p)
                if n is not None:
                    if p is not None:
                        pool.wait_ge(rstd_done, 2 * p + 2)
                    third_parts(n)
                if p is not None:
                    pool.wait_ge(rstd_done, 2 * p + 2)
                    if n is not None:
                        pool.wait_ge(p3_done, 2 * n + 2)
                    rstd(2 * p + 1)

            third_parts(0, first=True)
            run_turns(pool, turn)

        @block.tensor
        def _(pe):
            def sm_slot(t, key):
                pe.wait_ge(sm_free, t.uses("sm", key) + 1)
                return sm_bank[t.bank("sm", key, 3)]

            def r_slot(t, key):
                pe.wait_ge(r_free, t.uses("r", key) + 1)
                return r_bank[t.bank("r", key, 3)]

            m_read = {"t01": (ao_done, 4, 2), "t23": (ao_done, 4, 4), "aot": (comb_done, 2, 2), "wo": (r1_done, 1, 1),
                      "r1t": (xc_done, 2, 1), "h1t": (h1t_done, 2, 2), "gl": (gl_done, 1, 1), "gt": (gwt_done, 1, 1),
                      "r2t": (xc_done, 2, 2), "tok": (raw_done, 2, 2)}

            def m_slot(t, key):
                at = t.seq["m"].index(key)
                if at:
                    who, name = t.seq["m"][at - 1]
                    x = {"p": t.p, "a": t.a, "n": t.n}[who]
                elif t.kind == "prologue":
                    return
                elif t.kind == "first":
                    name, x = "tok", 0
                else:
                    name, x = "t01", t.p
                done, per, offset = m_read[name]
                pe.wait_ge(done, per * x + offset)

            def setup():
                pe.wait_ge(token_packed, 16)
                for g in range(16):
                    mm = pe.matmul((ot_bank, r_bank[0])[g // 8][0:64, 64 * (g % 8):64 * (g % 8) + 64],
                                   w("wt")[:, 64 * g:64 * g + 64], w("dft"), start=True, stop=True)
                mm.then_inc(mt_full, 1)
                pe.wait_ge(mt_read, 4)
                for kt in range(8):
                    mm = pe.transpose(m_bank[:, 64 * kt:64 * kt + 64], mt[:, 128 * kt:128 * kt + 128], ident[0:64, 0:64])
                mm.then_inc(wt_full, 1)
                pe.wait_ge(wt_read, 1)
                pe.wait_ge(ident_set, 1)
                pe.wait_ge(pool_set, 9)

            def tokens(t, k0=0, k1=8):
                if k0 == 0:
                    m_slot(t, ("n", "tok"))
                    pe.wait_ge(x_in, 64 * (t.n + 1))
                for kt in range(k0, k1):
                    for nn in range(2):
                        n0 = 8 * nn + kt // 4
                        mm = pe.matmul(m_bank[64 * nn:64 * nn + 64, :], wtok[:, kt, :],
                                       xs[:, n0:n0 + 8, V * (kt % 4):V * (kt % 4) + V],
                                       start=(kt == 0), stop=(kt == 7))
                if k1 == 8:
                    mm.then_inc(m_full, 1)

            def project_qk(t):
                pe.wait_ge(hc_done, 2 * t.n + 2)
                for c in range(2):
                    bank = sm_slot(t, ("n", "qk", c))
                    pe.matmul(bank[:, :], w("wqk"), hc[:, c * HALF:(c + 1) * HALF],
                              start=True, stop=True).then_inc(sm_full, 1)

            def project_v(t):
                bank = sm_slot(t, ("n", "vt"))
                for c in range(2):
                    mm = pe.matmul(bank[64 * c:64 * c + 64, :], w("wv"), hc[:, c * HALF:(c + 1) * HALF],
                                   start=True, stop=True)
                mm.then_inc(sm_full, 1)

            def turn_values(t):
                bank = sm_slot(t, ("n", "v"))
                pe.wait_ge(sm_free, t.uses("sm", ("n", "vt")) + 4)
                for i in range(4):
                    mm = pe.transpose(bank[:, 128 * i:128 * i + 128], vt[:, 128 * i:128 * i + 128], ident)
                mm.then_inc(sm_full, 1)

            def maxima(t, keys):
                for key in keys:
                    if key not in t.seq["sm"]:
                        continue
                    x = t.n if key[0] == "n" else t.a
                    bank = sm_slot(t, key)
                    if key[1] == "t":
                        pe.wait_ge(max_done, H * x + key[2] + 1)
                        pe.transpose(bank[0:NT, 0:128], ngm[:, key[2], :], ident).then_inc(sm_full, 1)
                        continue
                    h, m, c = key[2:]
                    if (h, m, c) == (0, 0, 0):
                        pe.wait_ge(stack01_in, 96 * (x + 1))
                    if (h, m, c) == (2, 0, 0):
                        pe.wait_ge(stack23_in, 96 * (x + 1))
                    pe.matmul(bank[:, :], qst[0:KS, h, 128 * m:128 * m + 128], kst[0:KS, h, c * HALF:(c + 1) * HALF],
                              start=True, stop=True).then_inc(sm_full, 1)

            def scores(t, s):
                h, m = s // NT, s % NT
                if m == 0:
                    pe.wait_ge(mrow_in, 16 * (H * t.a + h + 1))
                for c in range(2):
                    bank = r_slot(t, ("a", "st", s, c))
                    pe.matmul(bank[:, :], kst[0:KM, h, 128 * m:128 * m + 128], qst[0:KM, h, c * HALF:(c + 1) * HALF],
                              start=True, stop=True).then_inc(r_full, 1)

            def weigh(t, b, h, m):
                if b is t.p:
                    pe.wait_ge(r_free, t.uses("r") - 2 * (NT - 1 - m) + 3)
                else:
                    pe.wait_ge(r_free, t.uses("r", ("a", "st", NT * h + m, 1)) + 4)
                if m == 0:
                    if t.p is not None or h > 0:
                        pe.wait_ge(osb_done, H * b + h)
                    if h == 0:
                        pe.wait_ge(vv_done, b + 1)
                for j in range(4):
                    mm = pe.matmul(ot_bank[32 * j:32 * j + 32, 0:256], vv[:, m, h, :],
                                   pt[:, m % NPT, 256 * j:256 * j + 256], start=(m == 0), stop=(m == NT - 1),
                                   tile_position=(0, 32 * j))
                mm.then_inc(pv_done, 1)

            def turn_heads(t, who, pair):
                b = t.p if who == "p" else t.a
                m_slot(t, (who, ("t01", "t23")[pair]))
                pe.wait_ge(osb_done, H * b + 2 * pair + 2)
                for n in range(4):
                    mm = pe.transpose(m_bank[:, 128 * n:128 * n + 128],
                                      osb[:, 2 * pair + n // 2, 128 * (n % 2):128 * (n % 2) + 128], ident)
                mm.then_inc(m_full, 1)

            def turn_output(t):
                m_slot(t, ("p", "aot"))
                pe.wait_ge(ao_done, 4 * t.p + 4)
                for i in range(NT // 2):
                    mm = pe.transpose(m_bf[:, 128 * i:128 * i + 128],
                                      ao[:, 2 * i:2 * i + 2, :].rearrange("p a o -> p (a o)"), ident_bf[:, :])
                mm.then_inc(m_full, 1)

            def output(t):
                m_slot(t, ("p", "wo"))
                pe.wait_ge(res_done, t.p + 1)
                for c in range(2):
                    mm = pe.matmul(m_bank[64 * c:64 * c + 64, :], w("wo"), comb[:, c * HALF:(c + 1) * HALF],
                                   start=True, stop=True)
                mm.then_inc(m_full, 1)

            def turn_residual(t, name, src):
                m_slot(t, ("p", name))
                if name == "r1t":
                    pe.wait_ge(r1_done, t.p + 1)
                else:
                    pe.wait_ge(r_free, t.uses("r", ("p", "l3")) + 4)
                for c in range(4):
                    mm = pe.transpose(m_bank[:, 128 * c:128 * c + 128], src[:, 128 * c:128 * c + 128], ident)
                mm.then_inc(m_full, 1)

            def turn_h1(t):
                m_slot(t, ("p", "h1t"))
                pe.wait_ge(h1_done, t.p + 1)
                for c in range(4):
                    mm = pe.transpose(m_bank[:, 128 * c:128 * c + 128],
                                      h1[:, 2 * c:2 * c + 2, :].rearrange("p a o -> p (a o)"), ident)
                mm.then_inc(m_full, 1)

            def turn_logits(t):
                for i in range(NT):
                    mm = pe.transpose(m_bank[:, E * i:E * i + E], logits[:, 128 * i:128 * i + 128], ident[0:E, 0:E])
                mm.then_inc(m_full, 1)

            def turn_gates(t):
                m_slot(t, ("p", "gt"))
                pe.wait_ge(gw_done, t.p + 1)
                pe.transpose(m_bank[0:E * NT, 0:128], gw[:, :, :].rearrange("p e i -> p (e i)"), ident).then_inc(m_full, 1)

            def ffn_step(t, kind, ch):
                s = slice(ch * HALF, (ch + 1) * HALF)
                if kind == "s1":
                    pe.wait_ge(h1t_done, 2 * t.p + ch + 1)
                if kind == "s2":
                    pe.wait_ge(r_free, t.uses("r", ("p", "e3", ch)) + 4)
                bank = r_slot(t, ("p", kind, ch))
                if kind == "s1":
                    mm = pe.matmul(bank[0:64 + E, :], w("s1"), h1t[:, s], start=True, stop=True)
                elif kind[0] == "e":
                    e = int(kind[1])
                    mm = pe.matmul(bank[:, :], w("e1")[:, 128 * e:128 * e + 128], h1t[:, s], start=True, stop=True)
                elif kind == "s2":
                    mm = pe.matmul(bank[:, :], w("s2"), s1o[:, ch, :], start=True, stop=True)
                else:
                    for k in range(2):
                        e = 2 * int(kind[1]) + k
                        mm = pe.matmul(bank[64 * k:64 * k + 64, :], w("e2")[:, 64 * e:64 * e + 64], e1o[:, ch, e, :],
                                       start=True, stop=True)
                mm.then_inc(r_full, 1)

            def last_layer(t):
                bank = r_slot(t, ("p", "l3"))
                pe.wait_ge(gate_rows_in, 16 * (t.p + 1))
                pe.wait_ge(r_free, t.uses("r", ("p", "s2", 1)) + 4)
                for k in range(4):
                    if k == 2:
                        pe.wait_ge(e2g_done, 4 * t.p + 4)
                    for ch in range(2):
                        lhs = (w("w3"), w("s3"), w("e3")[:, 0:64], w("e3")[:, 64:128])[k]
                        rhs = (h1t[:, ch * HALF:(ch + 1) * HALF], s2o[:, ch, :], e2g[:, ch, 0, :], e2g[:, ch, 1, :])[k]
                        mm = pe.matmul(bank[64 * ch:64 * ch + 64, :], lhs, rhs, start=(k == 0), stop=(k == 3))
                mm.then_inc(r_full, 1)

            def of_p(t, s):
                if s == T23_AT:
                    turn_heads(t, "p", 1)
                if s == TURN_OUTPUT_AT:
                    turn_output(t)
                if s == OUTPUT_AT:
                    output(t)
                if s == R1T_AT:
                    turn_residual(t, "r1t", r1)
                if s == H1T_AT:
                    turn_h1(t)
                if s == t.gates_at:
                    turn_gates(t)
                if s == t.r2t_at:
                    turn_residual(t, "r2t", r2)

            def turn(t):
                for s in range(STAGES):
                    if t.a is not None:
                        scores(t, s)
                    if t.p is not None:
                        of_p(t, s)
                    if t.n is not None:
                        if s == V_AT:
                            project_v(t)
                        if s == VT_AT:
                            turn_values(t)
                    maxima(t, BESIDE[s][:1])
                    if t.p is not None:
                        if s == t.logits_at:
                            m_slot(t, ("p", "gl"))
                            pe.wait_ge(logits_done, 2 * t.p + 2)
                        for kind, ch in t.ffn_at.get(s, ()):
                            ffn_step(t, kind, ch)
                        if s == t.logits_at:
                            turn_logits(t)
                        if s == t.last_at:
                            last_layer(t)
                    maxima(t, BESIDE[s][1:2])
                    if t.n is not None:
                        if s in TOKEN_STAGES and t is not FIRST_TURN:
                            tokens(t, TOKEN_STAGES.index(s), TOKEN_STAGES.index(s) + TOKEN_STAGES.count(s))
                    if s % NT == 1 and s > NT and t.a is not None:
                        weigh(t, t.a, s // NT - 1, NT - 2)
                        weigh(t, t.a, s // NT - 1, NT - 1)
                    if s == 1 and t.p is not None:
                        weigh(t, t.p, H - 1, NT - 2)
                        weigh(t, t.p, H - 1, NT - 1)
                    if s % NT >= 2 and t.a is not None:
                        weigh(t, t.a, s // NT, s % NT - 2)
                    maxima(t, BESIDE[s][2:])
                    if s == QK_AT and t.n is not None:
                        project_qk(t)
                    if s == T01_AT and t.a is not None:
                        turn_heads(t, "a", 0)

            setup()
            tokens(PROLOGUE_TURN)
            pe.wait_ge(packed, 16)
            project_qk(PROLOGUE_TURN)
            project_v(PROLOGUE_TURN)
            turn_values(PROLOGUE_TURN)
            tokens(FIRST_TURN, 0, EARLY_TOKENS)
            for k in range(EARLY_TOKENS, 8):
                n = 2 * (k - EARLY_TOKENS)
                maxima(PROLOGUE_TURN, FIRST_MAX[n:n + 2])
                tokens(FIRST_TURN, k, k + 1)
            maxima(PROLOGUE_TURN, FIRST_MAX[2 * (8 - EARLY_TOKENS):])
            run_turns(pe, turn)

        @block.scalar
        def _(act):
            def raw_tokens(t):
                act.wait_ge(m_full, t.uses("m", ("n", "tok")) + 1)
                if t.a is not None:
                    act.wait_ge(res_done, t.a + 1)
                    act.wait_ge(hc_done, 2 * t.a + 2)
                for nn in range(2):
                    dst = raw[64:128, :].rearrange("p (i g v) -> p g i v", g=2, v=V)[:, nn]
                    act.activation(dst, m_bank[64 * nn:64 * nn + 64, :].rearrange("p (i v) -> p i v", v=V),
                                   ACT.Copy).then_inc(raw_done, 1)

            def first_parts(t):
                for c in range(2):
                    act.wait_ge(sm_full, t.uses("sm", ("n", "qk", c)) + 1)
                    bank = sm_bank[t.bank("sm", ("n", "qk", c), 3)]
                    act.activation(parts[:, 0, c * HALF:(c + 1) * HALF], bank[:, :], ACT.Copy).then_inc(p1_done, 1)

            def exponentials(t, s):
                for c in range(2):
                    if t.p is not None or s >= NPT:
                        act.wait_ge(pv_done, H * NT * t.a + s - NPT + 1)
                    key = ("a", "st", s, c)
                    act.wait_ge(r_full, t.uses("r", key) + 1)
                    act.activation(pt[:, s % NPT, c * HALF:(c + 1) * HALF], r_bank[t.bank("r", key, 3)][:, :], ACT.Exp,
                                   scale=SCALE).then_inc(r_free, 1)

            def turned_output(t):
                act.wait_ge(m_full, t.uses("m", ("p", "aot")) + 1)
                for k in range(2):
                    act.activation(comb[0:64, :].rearrange("p (i k n) -> p k i n", k=2, n=128)[:, k],
                                   m_bf[64 * k:64 * k + 64, 0:HALF].rearrange("p (i n) -> p i n", n=128),
                                   ACT.Copy).then_inc(comb_done, 1)

            def projected(t):
                act.wait_ge(m_full, t.uses("m", ("p", "wo")) + 1)
                act.activation(r1[:, :], m_bank[:, :], ACT.Identity, bias=w("bo")).then_inc(r1_done, 1)

            def squares(n):
                act.wait_ge(xc_done, n + 1)
                act.activation(sq[:, :, :], xc[:, :, :], ACT.Square).then_inc(sq_done, 1)

            def turned_h1(t):
                act.wait_ge(m_full, t.uses("m", ("p", "h1t")) + 1)
                for g in range(2):
                    act.activation(h1t[0:64, g * HALF:(g + 1) * HALF], m_bank[64 * g:64 * g + 64, :],
                                   ACT.Copy).then_inc(h1t_done, 1)

            def ffn_step(t, kind, ch):
                key = ("p", kind, ch)
                act.wait_ge(r_full, t.uses("r", key) + 1)
                bank = r_bank[t.bank("r", key, 3)]
                if kind == "s1":
                    dst, src, bias = s1o[0:64, ch, :], bank[0:64, :], 0.0
                    act.activation(logits[:, ch * HALF:(ch + 1) * HALF], bank[64:64 + E, :],
                                   ACT.Copy).then_inc(logits_done, 1)
                elif kind[0] == "e":
                    dst, src, bias = e1o[:, ch, int(kind[1]), :], bank[:, :], 0.0
                elif kind == "s2":
                    dst, src, bias = s2o[:, ch, :], bank[:, :], 0.0
                else:
                    k = int(kind[1])
                    dst, src, bias = e2o[:, ch, k, :], bank[:, :], w("eb2")[:, k:k + 1]
                act.activation(dst, src, ACT.Relu, bias=bias).then_inc(r_free, 1)

            def of_p(t, s):
                p = t.p
                for kind, ch in t.ffn_at.get(s, ()):
                    ffn_step(t, kind, ch)
                if s == TURN_OUTPUT_AT:
                    turned_output(t)
                if s == OUTPUT_AT:
                    projected(t)
                if s == R1T_AT:
                    squares(2 * p)
                if s == H1T_AT:
                    turned_h1(t)
                if s == t.logits_at:
                    act.wait_ge(gd_done, 2 * p + 1)
                    act.activation(ge[:, :, :], gd[:, :, :], ACT.Exp).then_inc(ge_done, 1)
                if s == t.share_at:
                    act.wait_ge(gd_done, 2 * p + 2)
                    act.activation(gu[:, :, :], gd[:, :, :], ACT.Exp).then_inc(gu_done, 1)
                if s == t.gates_at:
                    act.wait_ge(m_full, t.uses("m", ("p", "gt")) + 1)
                    act.activation(gwt[:, :], m_bank[0:E * NT, 0:128], ACT.Copy).then_inc(gwt_done, 1)
                if s == t.last_at:
                    key = ("p", "l3")
                    act.wait_ge(r_full, t.uses("r", key) + 1)
                    act.activation(r2[:, :], r_bank[t.bank("r", key, 3)][:, :], ACT.Copy).then_inc(r_free, 1)
                if s == t.r2t_at:
                    squares(2 * p + 1)

            def turn(t):
                for s in range(STAGES):
                    if t.a is not None:
                        exponentials(t, s)
                    if t.p is not None:
                        of_p(t, s)
                    if t.n is not None:
                        if s == TOKEN_STAGES[-1] and t is not FIRST_TURN:
                            raw_tokens(t)
                        if s == QK_AT:
                            first_parts(t)

            act.wait_ge(token_packed, 16)
            act.activation(ident_bf[:, :], ident, ACT.Copy).then_inc(ident_set, 1)
            act.wait_ge(mt_full, 1)
            for half in range(2):
                dst, src = token_weight_halves(1, half)
                act.activation(dst, src, ACT.Copy).then_inc(mt_read, 1)
            act.wait_ge(packed, 16)
            raw_tokens(PROLOGUE_TURN)
            first_parts(PROLOGUE_TURN)
            raw_tokens(FIRST_TURN)
            run_turns(act, turn)

        @block.vector
        def _(dve):
            taken = [0, 0, 0]

            def step(ins):
                taken[1] += 1
                ins.then_inc(dve_step, 1)
                dve.wait_ge(dve_step, DVE_STEPS * taken[2] + (taken[0] + taken[1]))

            def setup():
                dve.memset(later[:, :, 0:1], 3.0).then_inc(sm_free, 3)
                dve.memset(later[:, :, 1:2], 2.0).then_inc(r_free, 3)
                dve.memset(later[:, :, 2:3], 1.0).then_inc(y_out, 1)
                step(dve.memset(later[:, :, 3:4], 0.0))
                dve.wait_ge(mt_full, 1)
                for half in range(2):
                    dst, src = token_weight_halves(0, half)
                    dve.tensor_copy(dst, src).then_inc(mt_read, 1)
                dve.wait_ge(wt_full, 1)
                dve.tensor_copy(wtok[:, :, :].rearrange("p k o -> p (k o)"), m_bank[:, :]).then_inc(wt_read, 1)
                dve.wait_ge(pool_set, 9)

            def clip(t):
                dve.wait_ge(raw_done, 2 * t.n + 2)
                for c in range(2):
                    s = slice(c * HALF, (c + 1) * HALF)
                    dve.tensor_scalar(hc[0:64, s], raw[64:128, s], CLIP, -CLIP, ALU.min, ALU.max).then_inc(hc_done, 1)

            def rest_of(t, c):
                s = slice(c * HALF, (c + 1) * HALF)
                key = ("n", "qk", c)
                dve.wait_ge(p1_done, 2 * t.n + c + 1)
                dve.tensor_tensor(rest[:, s], sm_bank[t.bank("sm", key, 3)][:, :], parts[:, 0, s],
                                  ALU.subtract).then_inc(sm_free, 1)
                dve.wait_ge(sm_free, t.uses("sm", key) + 4)
                dve.tensor_copy(parts[:, 1, s], rest[:, s]).then_inc(p2_done, 1)

            def kept_values(t):
                key = ("n", "vt")
                dve.wait_ge(sm_full, t.uses("sm", key) + 1)
                dve.tensor_copy(vt[:, :], sm_bank[t.bank("sm", key, 3)][:, :]).then_inc(sm_free, 1)

            def values(t):
                key = ("n", "v")
                dve.wait_ge(sm_full, t.uses("sm", key) + 1)
                dve.tensor_copy(vst[:, :, :].rearrange("p (g i) d -> p i g d", g=2),
                                sm_bank[t.bank("sm", key, 3)][:, :].rearrange("p (i g d) -> p i g d", g=2, d=D)
                                ).then_inc(sm_free, 1)

            def max_tile(t, key):
                h, m, c = key[2:]
                dve.wait_ge(sm_full, t.uses("sm", key) + 1)
                dve.tensor_reduce(mx2[:, h, m, c:c + 1], sm_bank[t.bank("sm", key, 3)][:, :], AX.X, ALU.max).then_inc(sm_free, 1)
                if (m, c) == (NT - 1, 1):
                    dve.wait_ge(sm_free, t.uses("sm", key) + 4)
                    dve.tensor_reduce(ngm[:, h, :], mx2[:, h, :, :], AX.X, ALU.max, negate=True).then_inc(max_done, 1)

            def split_max(t, key):
                h = key[2]
                bank = sm_bank[t.bank("sm", key, 3)][0:NT, 0:128]
                dve.wait_ge(sm_full, t.uses("sm", key) + 1)
                step(dve.tensor_copy(mpart[:, h % 2, 0, :], bank))
                dve.tensor_tensor(mrest[:, :], bank, mpart[:, h % 2, 0, :], ALU.subtract).then_inc(sm_free, 1)
                dve.wait_ge(sm_free, t.uses("sm", key) + 4)
                step(dve.tensor_copy(mpart[:, h % 2, 1, :], mrest[:, :]))
                dve.tensor_tensor(mpart[:, h % 2, 2, :], mrest[:, :], mpart[:, h % 2, 1, :],
                                  ALU.subtract).then_inc(mpart_done, 1)

            def maxima(t, keys):
                for key in keys:
                    if key in t.seq["sm"]:
                        (split_max if key[1] == "t" else max_tile)(t, key)

            def head_out(b, h):
                dve.wait_ge(pv_done, H * NT * b + NT * (h + 1))
                dve.tensor_copy(osb[:, h, :], ot_bank[:, 0:256]).then_inc(osb_done, 1)

            def divide(t, who, p):
                b = t.p if who == "p" else t.a
                dve.wait_ge(m_full, t.uses("m", (who, ("t01", "t23")[p])) + 1)
                turned = m_bank[:, :].rearrange("p (k a j d) -> p k a j d", k=2, a=2, j=4)
                step(dve.reciprocal(rec[:, p, :, :].rearrange("p k n -> p (k n)"),
                                       m_bank[:, :].rearrange("p (n d) -> p n d", d=32)[:, :, DH]))
                for k in range(2):
                    h = 2 * p + k
                    dst = ao[:, :, DH * h:DH * h + DH].rearrange("p (j a) d -> p a j d", a=2)
                    dve.tensor_tensor(dst, turned[:, k, :, :, 0:DH],
                                      rec[:, p, k, :].rearrange("p (a j) -> p a j", a=2).unsqueeze(3)
                                      .to_broadcast([128, 2, 4, DH]), ALU.mult).then_inc(ao_done, 1)

            def spread(v):
                return v.unsqueeze(2).to_broadcast([128, NT, D])

            def centre(t, name):
                dve.wait_ge(m_full, t.uses("m", ("p", name)) + 1)
                r = m_bank[:, :].rearrange("p (g o) -> p g o", o=D)
                step(dve.tensor_reduce(st[:, 0, :], r, AX.X, ALU.add))
                dve.scalar_tensor_tensor(out=xc[:, :, :], in0=spread(st[:, 0, :]), scalar=-1.0 / D, in1=r,
                                         op0=ALU.mult, op1=ALU.add).then_inc(xc_done, 1)

            def variance(n):
                dve.wait_ge(sq_done, n + 1)
                step(dve.tensor_reduce(st[:, 2, :], sq[:, :, :], AX.X, ALU.add))
                dve.tensor_scalar(st[:, 3, :], st[:, 2, :], 1.0 / D, EPS, ALU.mult, ALU.add).then_inc(var_done, 1)

            def first_norm(b):
                dve.wait_ge(rstd_done, 2 * b + 2)
                dve.tensor_tensor(h1[:, :, :], xc[:, :, :], spread(st[:, 4, :]), ALU.mult).then_inc(h1_done, 1)

            def second_norm(b):
                dve.wait_ge(rstd_done, 2 * b + 3)
                dve.wait_ge(y_out, 32 * b + 1)
                dve.tensor_tensor(y[:, :, :].rearrange("p (a c) o -> p c a o", a=2),
                                  xc[:, :, :].rearrange("p (c a) o -> p c a o", a=2),
                                  st[:, 4, :].rearrange("p (c a) -> p c a", a=2).unsqueeze(3)
                                  .to_broadcast([128, 4, 2, D]), ALU.mult).then_inc(y_done, 1)

            def over(v):
                return v.unsqueeze(2).to_broadcast([128, NT, E])

            def less_maximum(t):
                b = t.p
                dve.wait_ge(m_full, t.uses("m", ("p", "gl")) + 1)
                dve.tensor_copy(gl[:, :, :].rearrange("p i e -> p (i e)"), m_bank[:, 0:NT * E]).then_inc(gl_done, 1)
                dve.wait_ge(gl_done, b + 1)
                step(dve.tensor_reduce(gs[:, 0, :], gl[:, :, :], AX.X, ALU.max))
                dve.tensor_tensor(gd[:, :, :], gl[:, :, :], over(gs[:, 0, :]), ALU.subtract).then_inc(gd_done, 1)

            def shares(b):
                dve.wait_ge(ge_done, b + 1)
                step(dve.tensor_reduce(gs[:, 1, :], ge[:, :, :], AX.X, ALU.add))
                step(dve.reciprocal(gs[:, 2, :], gs[:, 1, :]))
                step(dve.tensor_tensor(gp[:, :, :], ge[:, :, :], over(gs[:, 2, :]), ALU.mult))
                step(dve.tensor_reduce(gs[:, 3, :], gp[:, :, :], AX.X, ALU.max))
                dve.tensor_tensor(gd[:, :, :], gp[:, :, :], over(gs[:, 3, :]), ALU.subtract).then_inc(gd_done, 1)

            def rank_gates():
                for k in range(1, E):
                    step(dve.tensor_tensor(gc[:, k, :, 0:E - k], gp[:, :, 0:E - k], gp[:, :, k:E], ALU.is_ge))
                for k in range(1, E):
                    if k == 1:
                        step(dve.tensor_tensor(rank[:, :, 0:E - 1], later[:, :, 0:E - 1], gc[:, 1, :, 0:E - 1],
                                                  ALU.subtract))
                        step(dve.tensor_copy(rank[:, :, E - 1:E], later[:, :, E - 1:E]))
                    else:
                        step(dve.tensor_tensor(rank[:, :, 0:E - k], rank[:, :, 0:E - k], gc[:, k, :, 0:E - k],
                                                  ALU.subtract))
                    step(dve.tensor_tensor(rank[:, :, k:E], rank[:, :, k:E], gc[:, k, :, 0:E - k], ALU.add))

            def choose(b):
                dve.wait_ge(gu_done, b + 1)
                step(dve.scalar_tensor_tensor(out=gm[:, :, :], in0=rank[:, :, :], scalar=2.0, in1=gu[:, :, :],
                                                 op0=ALU.is_lt, op1=ALU.mult))
                step(dve.tensor_reduce(gs[:, 4, :], gm[:, :, :], AX.X, ALU.add))
                step(dve.reciprocal(gs[:, 5, :], gs[:, 4, :]))
                dve.tensor_tensor(gw[:, :, :].rearrange("p e i -> p i e"), gm[:, :, :], over(gs[:, 5, :]),
                                  ALU.mult).then_inc(gw_done, 1)

            def weigh_experts(t, ch):
                b = t.p
                if ch == 0:
                    dve.wait_ge(gate_in, 64 * (b + 1))
                for k in range(2):
                    dve.wait_ge(r_free, t.uses("r", ("p", f"p{k}", ch)) + 4)
                    dve.tensor_tensor(e2g[:, ch, k, :], e2o[:, ch, k, :], wgb[:, k, ch * HALF:(ch + 1) * HALF],
                                      ALU.mult).then_inc(e2g_done, 1)

            def of_p(t, s):
                p = t.p
                if s == 2:
                    head_out(p, H - 1)
                if s == T23_AT:
                    divide(t, "p", 1)
                if s == R1T_AT:
                    centre(t, "r1t")
                if s == VAR1_AT:
                    variance(2 * p)
                if s == NORM1_AT:
                    first_norm(p)
                if s == LOGITS_AT:
                    less_maximum(t)
                if s == SHARE_AT:
                    shares(p)
                if s == RANK_AT:
                    rank_gates()
                if s == CHOOSE_AT:
                    choose(p)
                if s in WEIGH_AT:
                    weigh_experts(t, WEIGH_AT[s])
                if s == R2T_AT:
                    centre(t, "r2t")
                if s == VAR2_AT:
                    variance(2 * p + 1)
                if s == NORM2_AT:
                    second_norm(p)

            def turn(t):
                taken[:] = taken[0] + taken[1], 0, (t.p if t.kind == "loop" else 0)
                if t.kind == "last":
                    taken[0] += DVE_STEPS * (B - 3)
                for s in range(STAGES):
                    if t.p is not None:
                        of_p(t, s)
                    if t.n is not None and s == CLIP_AT:
                        clip(t)
                    if s % NT == 2 and s > NT and t.a is not None:
                        head_out(t.a, s // NT - 1)
                    if t.n is not None:
                        if s == V_AT:
                            kept_values(t)
                        if s == VT_AT:
                            values(t)
                    maxima(t, BESIDE[s])
                    if t.n is not None:
                        if s == QK_AT:
                            rest_of(t, 0)
                            rest_of(t, 1)
                    if s == T01_AT and t.a is not None:
                        divide(t, "a", 0)
                assert t.kind != "loop" or taken[1] == DVE_STEPS, taken[1]

            setup()
            clip(PROLOGUE_TURN)
            rest_of(PROLOGUE_TURN, 0)
            rest_of(PROLOGUE_TURN, 1)
            kept_values(PROLOGUE_TURN)
            values(PROLOGUE_TURN)
            maxima(PROLOGUE_TURN, FIRST_MAX)
            run_turns(dve, turn)


def packed_weights(a):
    import numpy as np

    pack = np.zeros((128, PACK_COLS), np.float32)

    def put(name, value, r0=0, c0=0):
        value = np.asarray(value)
        at = PACK[name][1]
        pack[r0:r0 + value.shape[0], at + c0:at + c0 + value.shape[1]] = value

    by_dim = np.arange(D).reshape(H, DH).T.reshape(-1)
    put("ident", np.eye(128))
    for n, k in enumerate("qk"):
        put("wqk", a[f"L0_attn_W{k}"][by_dim].T, 0, D * n)
        put("wqk", a[f"L0_attn_b{k}"][by_dim][None], D, D * n)
    put("wv", a["L0_attn_Wv"].T)
    put("wv", a["L0_attn_bv"][None], D)
    put("wo", a["L0_attn_Wo"].T)
    put("wo", np.eye(D), D)
    put("bo", a["L0_attn_bo"][:, None])
    put("bo", a["L0_attn_bo"][:, None], D)
    put("s1", a["L0_ffn_sW1"])
    put("s1", a["L0_ffn_sb1"][None], D)
    put("s1", a["L0_ffn_gW"], 0, D)
    put("s1", a["L0_ffn_gb"][None], D, D)
    put("s2", a["L0_ffn_sW2"])
    put("s2", a["L0_ffn_sb2"][None], D)
    put("s3", a["L0_ffn_sW3"])
    put("w3", np.eye(D))
    put("w3", a["L0_ffn_sb3"][None], D)
    put("w3", a["L0_ffn_eb3"], GATE_ROW)
    for e in range(E):
        put("e1", a["L0_ffn_eW1"][e], 0, 128 * e)
        put("e1", a["L0_ffn_eb1"][e][None], D, 128 * e)
        put("e2", a["L0_ffn_eW2"][e], 0, 64 * e)
        put("eb2", a["L0_ffn_eb2"][e][:, None], 64 * (e % 2), e // 2)
        put("e3", a["L0_ffn_eW3"][e], 64 * (e % 2), 64 * (e // 2))
    angle = 2 * np.pi * np.arange(RF // 2)[:, None] * np.arange(PATCH)[None] / PATCH
    dft = np.concatenate([np.cos(angle), -np.sin(angle)]) / np.sqrt(PATCH)
    dft[np.abs(dft) < 1e-12] = 0.0
    tok = a["L0_tok_W"].reshape(D, RF, C // CG, CG)
    for c in range(CG):
        put("dft", dft, RF * c, PATCH * c)
        put("wt", tok[:, :, :, c].transpose(1, 2, 0).reshape(RF, -1), RF * c)
    return pack


def kernel(**inputs):
    import numpy as np
    import concourse.bacc as bacc
    from concourse.bass_utils import run_bass_kernel_spmd

    a = {k: np.asarray(v) for k, v in inputs.items()}
    arrays = {"x": np.ascontiguousarray(a["x"]), "pack": packed_weights(a)}
    nc = bacc.Bacc("TRN2", target_bir_lowering=False, num_devices=1)
    args = [nc.dram_tensor(n, v.shape, mybir.dt.from_np(v.dtype), kind="ExternalInput").ap() for n, v in arrays.items()]
    out = nc.dram_tensor("out", (B, N, D), F32, kind="ExternalOutput").ap()
    vit_layer(nc, *args, out)
    r = run_bass_kernel_spmd(nc, [arrays], core_ids=[0])
    return r.results[0]["out"]
```
